# Optimizing a Trainium2 kernel written in Bass

```python
import numpy as np
import jax
import jax.numpy as jnp

def _softmax(x, axis=-1):
    return jax.nn.softmax(x, axis=axis)

def _gelu(x):
    return jax.nn.gelu(x, approximate=True)

def _silu(x):
    return jax.nn.silu(x)

def _sigmoid(x):
    return jax.nn.sigmoid(x)

def _layernorm(x, axis=-1, eps=1e-05):
    m = jnp.mean(x, axis=axis, keepdims=True)
    v = jnp.var(x, axis=axis, keepdims=True)
    return (x - m) / jnp.sqrt(v + eps)

def _scatter_add(tgt, idx, src, axis=0):
    return tgt.at[idx].add(src)

def _segment_sum(src, seg, n):
    return jax.ops.segment_sum(src, seg, n)
kernel_name = 'mk_dlrm_tower_d1_rec_r8_ed98fe'

def setup_inputs(seed: int=0):
    np.random.seed(seed)
    _w = jnp.asarray

    def _rec_inputs():
        import jax
        import jax.numpy as jnp
        _tk = jax.random.key(seed)
        dense_ctx = jax.random.normal(jax.random.fold_in(_tk, 190), (2048, 16), jnp.float32)
        ids = jnp.stack([jax.random.randint(jax.random.fold_in(_tk, 200 + f), (2048,), 0, v, jnp.int32) for f, v in enumerate([12500, 12500, 12500, 1250, 1000, 1000, 125000, 1000, 125000, 125000, 125000, 12500, 1250, 12500, 1000, 1250, 1250, 1250, 125000, 12500, 1000, 125000, 125000, 1250, 125000, 1000, 1000, 12500, 1000, 1000, 12500, 125000, 1000, 1250, 1000, 1000, 1000, 125000, 1000])], axis=1)
        tbl_0 = 0.05 * jax.random.normal(jax.random.fold_in(_tk, 500 + 0), (12500, 16), jnp.float32)
        tbl_1 = 0.05 * jax.random.normal(jax.random.fold_in(_tk, 500 + 1), (12500, 16), jnp.float32)
        tbl_2 = 0.05 * jax.random.normal(jax.random.fold_in(_tk, 500 + 2), (12500, 16), jnp.float32)
        tbl_3 = 0.05 * jax.random.normal(jax.random.fold_in(_tk, 500 + 3), (1250, 16), jnp.float32)
        tbl_4 = 0.05 * jax.random.normal(jax.random.fold_in(_tk, 500 + 4), (1000, 16), jnp.float32)
        tbl_5 = 0.05 * jax.random.normal(jax.random.fold_in(_tk, 500 + 5), (1000, 16), jnp.float32)
        tbl_6 = 0.05 * jax.random.normal(jax.random.fold_in(_tk, 500 + 6), (125000, 16), jnp.float32)
        tbl_7 = 0.05 * jax.random.normal(jax.random.fold_in(_tk, 500 + 7), (1000, 16), jnp.float32)
        tbl_8 = 0.05 * jax.random.normal(jax.random.fold_in(_tk, 500 + 8), (125000, 16), jnp.float32)
        tbl_9 = 0.05 * jax.random.normal(jax.random.fold_in(_tk, 500 + 9), (125000, 16), jnp.float32)
        tbl_10 = 0.05 * jax.random.normal(jax.random.fold_in(_tk, 500 + 10), (125000, 16), jnp.float32)
        tbl_11 = 0.05 * jax.random.normal(jax.random.fold_in(_tk, 500 + 11), (12500, 16), jnp.float32)
        tbl_12 = 0.05 * jax.random.normal(jax.random.fold_in(_tk, 500 + 12), (1250, 16), jnp.float32)
        tbl_13 = 0.05 * jax.random.normal(jax.random.fold_in(_tk, 500 + 13), (12500, 16), jnp.float32)
        tbl_14 = 0.05 * jax.random.normal(jax.random.fold_in(_tk, 500 + 14), (1000, 16), jnp.float32)
        tbl_15 = 0.05 * jax.random.normal(jax.random.fold_in(_tk, 500 + 15), (1250, 16), jnp.float32)
        tbl_16 = 0.05 * jax.random.normal(jax.random.fold_in(_tk, 500 + 16), (1250, 16), jnp.float32)
        tbl_17 = 0.05 * jax.random.normal(jax.random.fold_in(_tk, 500 + 17), (1250, 16), jnp.float32)
        tbl_18 = 0.05 * jax.random.normal(jax.random.fold_in(_tk, 500 + 18), (125000, 16), jnp.float32)
        tbl_19 = 0.05 * jax.random.normal(jax.random.fold_in(_tk, 500 + 19), (12500, 16), jnp.float32)
        tbl_20 = 0.05 * jax.random.normal(jax.random.fold_in(_tk, 500 + 20), (1000, 16), jnp.float32)
        tbl_21 = 0.05 * jax.random.normal(jax.random.fold_in(_tk, 500 + 21), (125000, 16), jnp.float32)
        tbl_22 = 0.05 * jax.random.normal(jax.random.fold_in(_tk, 500 + 22), (125000, 16), jnp.float32)
        tbl_23 = 0.05 * jax.random.normal(jax.random.fold_in(_tk, 500 + 23), (1250, 16), jnp.float32)
        tbl_24 = 0.05 * jax.random.normal(jax.random.fold_in(_tk, 500 + 24), (125000, 16), jnp.float32)
        tbl_25 = 0.05 * jax.random.normal(jax.random.fold_in(_tk, 500 + 25), (1000, 16), jnp.float32)
        tbl_26 = 0.05 * jax.random.normal(jax.random.fold_in(_tk, 500 + 26), (1000, 16), jnp.float32)
        tbl_27 = 0.05 * jax.random.normal(jax.random.fold_in(_tk, 500 + 27), (12500, 16), jnp.float32)
        tbl_28 = 0.05 * jax.random.normal(jax.random.fold_in(_tk, 500 + 28), (1000, 16), jnp.float32)
        tbl_29 = 0.05 * jax.random.normal(jax.random.fold_in(_tk, 500 + 29), (1000, 16), jnp.float32)
        tbl_30 = 0.05 * jax.random.normal(jax.random.fold_in(_tk, 500 + 30), (12500, 16), jnp.float32)
        tbl_31 = 0.05 * jax.random.normal(jax.random.fold_in(_tk, 500 + 31), (125000, 16), jnp.float32)
        tbl_32 = 0.05 * jax.random.normal(jax.random.fold_in(_tk, 500 + 32), (1000, 16), jnp.float32)
        tbl_33 = 0.05 * jax.random.normal(jax.random.fold_in(_tk, 500 + 33), (1250, 16), jnp.float32)
        tbl_34 = 0.05 * jax.random.normal(jax.random.fold_in(_tk, 500 + 34), (1000, 16), jnp.float32)
        tbl_35 = 0.05 * jax.random.normal(jax.random.fold_in(_tk, 500 + 35), (1000, 16), jnp.float32)
        tbl_36 = 0.05 * jax.random.normal(jax.random.fold_in(_tk, 500 + 36), (1000, 16), jnp.float32)
        tbl_37 = 0.05 * jax.random.normal(jax.random.fold_in(_tk, 500 + 37), (125000, 16), jnp.float32)
        tbl_38 = 0.05 * jax.random.normal(jax.random.fold_in(_tk, 500 + 38), (1000, 16), jnp.float32)
        _rk = jax.random.fold_in(_tk, 7)
        W_top1 = 0.0606339 * jax.random.normal(jax.random.fold_in(_tk, 801), (272, 512), jnp.float32)
        W_top2 = 0.0441942 * jax.random.normal(jax.random.fold_in(_tk, 802), (512, 256), jnp.float32)
        W_top3 = 0.0625 * jax.random.normal(jax.random.fold_in(_tk, 803), (256, 1), jnp.float32)
        b_top1 = jnp.zeros((512,), jnp.float32)
        b_top2 = jnp.zeros((256,), jnp.float32)
        return (dense_ctx, ids, tbl_0, tbl_1, tbl_2, tbl_3, tbl_4, tbl_5, tbl_6, tbl_7, tbl_8, tbl_9, tbl_10, tbl_11, tbl_12, tbl_13, tbl_14, tbl_15, tbl_16, tbl_17, tbl_18, tbl_19, tbl_20, tbl_21, tbl_22, tbl_23, tbl_24, tbl_25, tbl_26, tbl_27, tbl_28, tbl_29, tbl_30, tbl_31, tbl_32, tbl_33, tbl_34, tbl_35, tbl_36, tbl_37, tbl_38, W_top1, b_top1, W_top2, b_top2, W_top3)
    dense_ctx, ids, tbl_0, tbl_1, tbl_2, tbl_3, tbl_4, tbl_5, tbl_6, tbl_7, tbl_8, tbl_9, tbl_10, tbl_11, tbl_12, tbl_13, tbl_14, tbl_15, tbl_16, tbl_17, tbl_18, tbl_19, tbl_20, tbl_21, tbl_22, tbl_23, tbl_24, tbl_25, tbl_26, tbl_27, tbl_28, tbl_29, tbl_30, tbl_31, tbl_32, tbl_33, tbl_34, tbl_35, tbl_36, tbl_37, tbl_38, W_top1, b_top1, W_top2, b_top2, W_top3 = _rec_inputs()

    def _L0_rec_setup():
        import jax, jax.numpy as jnp
        import numpy as np
        LAYER_SIZES = [128, 128, 128]
        F0 = 39
        D = 16
        B = 256
        key = jax.random.key(seed)
        ks = jax.random.split(key, 4)
        field_nums = [F0, LAYER_SIZES[0] // 2, LAYER_SIZES[1] // 2]
        x = jax.random.normal(ks[0], (B, F0, D), dtype=jnp.float32)
        W0 = jax.random.normal(ks[1], (F0 * field_nums[0], LAYER_SIZES[0]), dtype=jnp.float32) * 0.05
        W1 = jax.random.normal(ks[2], (F0 * field_nums[1], LAYER_SIZES[1]), dtype=jnp.float32) * 0.05
        W2 = jax.random.normal(ks[3], (F0 * field_nums[2], LAYER_SIZES[2]), dtype=jnp.float32) * 0.05
        b0 = jnp.zeros((LAYER_SIZES[0],), jnp.float32)
        b1 = jnp.zeros((LAYER_SIZES[1],), jnp.float32)
        b2 = jnp.zeros((LAYER_SIZES[2],), jnp.float32)
        return {'x': x, 'W0': W0, 'W1': W1, 'W2': W2, 'b0': b0, 'b1': b1, 'b2': b2}
    _L0_rec_all = _L0_rec_setup()
    _L0_rec_in = {k: v for k, v in _L0_rec_all.items() if k in ('W0', 'W1', 'W2', 'b0', 'b1', 'b2')}
    del _L0_rec_all
    return {'dense_ctx': dense_ctx, 'ids': ids, 'tbl_0': tbl_0, 'tbl_1': tbl_1, 'tbl_2': tbl_2, 'tbl_3': tbl_3, 'tbl_4': tbl_4, 'tbl_5': tbl_5, 'tbl_6': tbl_6, 'tbl_7': tbl_7, 'tbl_8': tbl_8, 'tbl_9': tbl_9, 'tbl_10': tbl_10, 'tbl_11': tbl_11, 'tbl_12': tbl_12, 'tbl_13': tbl_13, 'tbl_14': tbl_14, 'tbl_15': tbl_15, 'tbl_16': tbl_16, 'tbl_17': tbl_17, 'tbl_18': tbl_18, 'tbl_19': tbl_19, 'tbl_20': tbl_20, 'tbl_21': tbl_21, 'tbl_22': tbl_22, 'tbl_23': tbl_23, 'tbl_24': tbl_24, 'tbl_25': tbl_25, 'tbl_26': tbl_26, 'tbl_27': tbl_27, 'tbl_28': tbl_28, 'tbl_29': tbl_29, 'tbl_30': tbl_30, 'tbl_31': tbl_31, 'tbl_32': tbl_32, 'tbl_33': tbl_33, 'tbl_34': tbl_34, 'tbl_35': tbl_35, 'tbl_36': tbl_36, 'tbl_37': tbl_37, 'tbl_38': tbl_38, 'W_top1': W_top1, 'b_top1': b_top1, 'W_top2': W_top2, 'b_top2': b_top2, 'W_top3': W_top3, 'L0_rec_W0': _L0_rec_in['W0'], 'L0_rec_W1': _L0_rec_in['W1'], 'L0_rec_W2': _L0_rec_in['W2'], 'L0_rec_b0': _L0_rec_in['b0'], 'L0_rec_b1': _L0_rec_in['b1'], 'L0_rec_b2': _L0_rec_in['b2']}

def reference(dense_ctx, ids, tbl_0, tbl_1, tbl_2, tbl_3, tbl_4, tbl_5, tbl_6, tbl_7, tbl_8, tbl_9, tbl_10, tbl_11, tbl_12, tbl_13, tbl_14, tbl_15, tbl_16, tbl_17, tbl_18, tbl_19, tbl_20, tbl_21, tbl_22, tbl_23, tbl_24, tbl_25, tbl_26, tbl_27, tbl_28, tbl_29, tbl_30, tbl_31, tbl_32, tbl_33, tbl_34, tbl_35, tbl_36, tbl_37, tbl_38, W_top1, b_top1, W_top2, b_top2, W_top3, L0_rec_W0, L0_rec_W1, L0_rec_W2, L0_rec_b0, L0_rec_b1, L0_rec_b2):
    import jax
    import jax.numpy as jnp

    def _L0_rec_ref(x, W0, W1, W2, b0, b1, b2):
        import jax, jax.numpy as jnp
        import numpy as np
        LAYER_SIZES = [128, 128, 128]
        F0 = 39
        D = 16
        B = 256
        Ws = [W0, W1, W2]
        bs = [b0, b1, b2]
        h = x
        outs = []
        n_layers = len(LAYER_SIZES)
        for i, S in enumerate(LAYER_SIZES):
            Fk = h.shape[1]
            Wr = Ws[i].reshape(F0, Fk, S)
            out = jax.nn.relu(jnp.einsum('bfd,bgd,fgs->bsd', x, h, Wr) + bs[i][None, :, None])
            if i != n_layers - 1:
                h, direct = (out[:, :S // 2], out[:, S // 2:])
            else:
                direct = out
            outs.append(direct)
        result = jnp.concatenate(outs, axis=1)
        return jnp.sum(result, axis=-1)
    e = jnp.stack([tbl_0[ids[:, 0]], tbl_1[ids[:, 1]], tbl_2[ids[:, 2]], tbl_3[ids[:, 3]], tbl_4[ids[:, 4]], tbl_5[ids[:, 5]], tbl_6[ids[:, 6]], tbl_7[ids[:, 7]], tbl_8[ids[:, 8]], tbl_9[ids[:, 9]], tbl_10[ids[:, 10]], tbl_11[ids[:, 11]], tbl_12[ids[:, 12]], tbl_13[ids[:, 13]], tbl_14[ids[:, 14]], tbl_15[ids[:, 15]], tbl_16[ids[:, 16]], tbl_17[ids[:, 17]], tbl_18[ids[:, 18]], tbl_19[ids[:, 19]], tbl_20[ids[:, 20]], tbl_21[ids[:, 21]], tbl_22[ids[:, 22]], tbl_23[ids[:, 23]], tbl_24[ids[:, 24]], tbl_25[ids[:, 25]], tbl_26[ids[:, 26]], tbl_27[ids[:, 27]], tbl_28[ids[:, 28]], tbl_29[ids[:, 29]], tbl_30[ids[:, 30]], tbl_31[ids[:, 31]], tbl_32[ids[:, 32]], tbl_33[ids[:, 33]], tbl_34[ids[:, 34]], tbl_35[ids[:, 35]], tbl_36[ids[:, 36]], tbl_37[ids[:, 37]], tbl_38[ids[:, 38]]], axis=1)
    z = _L0_rec_ref(e, L0_rec_W0, L0_rec_W1, L0_rec_W2, L0_rec_b0, L0_rec_b1, L0_rec_b2)
    z = z.reshape(z.shape[0], -1)
    h = jnp.concatenate([z, dense_ctx], axis=1)
    h = jnp.maximum(h @ W_top1 + b_top1, 0.0)
    h = jnp.maximum(h @ W_top2 + b_top2, 0.0)
    y = h @ W_top3
    return y

_drawn_inputs = setup_inputs


def setup_inputs(seed=0):
    import zlib

    import numpy as np

    out = dict(_drawn_inputs(seed))
    spreads = {'b_top1': (0.0, 0.8),
     'b_top2': (0.0, 0.8),
     'L0_rec_b0': (0.0, 0.301),
     'L0_rec_b1': (0.0, 0.451),
     'L0_rec_b2': (0.0, 0.313)}
    factors = {'tbl_0': 8.0,
     'tbl_1': 8.0,
     'tbl_2': 8.0,
     'tbl_3': 8.0,
     'tbl_4': 8.0,
     'tbl_5': 8.0,
     'tbl_6': 8.0,
     'tbl_7': 8.0,
     'tbl_8': 8.0,
     'tbl_9': 8.0,
     'tbl_10': 8.0,
     'tbl_11': 8.0,
     'tbl_12': 8.0,
     'tbl_13': 8.0,
     'tbl_14': 8.0,
     'tbl_15': 8.0,
     'tbl_16': 8.0,
     'tbl_17': 8.0,
     'tbl_18': 8.0,
     'tbl_19': 8.0,
     'tbl_20': 8.0,
     'tbl_21': 8.0,
     'tbl_22': 7.096,
     'tbl_23': 8.0,
     'tbl_24': 8.0,
     'tbl_25': 8.0,
     'tbl_26': 7.488,
     'tbl_27': 8.0,
     'tbl_28': 8.0,
     'tbl_29': 8.0,
     'tbl_30': 8.0,
     'tbl_31': 7.348,
     'tbl_32': 8.0,
     'tbl_33': 8.0,
     'tbl_34': 8.0,
     'tbl_35': 8.0,
     'tbl_36': 8.0,
     'tbl_37': 8.0,
     'tbl_38': 8.0,
     'L0_rec_W0': 6.509,
     'L0_rec_W1': 3.254,
     'dense_ctx': 5.708}
    for name, (base, spread) in spreads.items():
        noise = np.random.default_rng([zlib.crc32(name.encode()), seed]).standard_normal(out[name].shape)
        drawn = base * np.exp(spread * noise) if base else spread * noise
        out[name] = jnp.asarray(drawn.astype(out[name].dtype))
    for name, factor in factors.items():
        out[name] = (out[name] * factor).astype(out[name].dtype)
    return out
```

```python
from contextlib import ExitStack

import concourse.bass as bass
from concourse import mybir

F32 = mybir.dt.float32
U32 = mybir.dt.uint32
ALU = mybir.AluOpType
ACT = mybir.ActivationFunctionType
AX = mybir.AxisListType

FIELDS, DIM, BATCH = 39, 16, 2048
P = 128
HALF = 64
TILE = 512
BLOCKS = BATCH // P
D_PER_TILE = TILE // P
TILES = DIM // D_PER_TILE
COLS = BATCH * DIM
SHIFTS = FIELDS // 2 + 1
PAIR_CHUNKS = 7
PAIR_GROUPS = 3
PAIR_ROWS = PAIR_GROUPS * FIELDS
WIDE_CHUNKS = (FIELDS + 1) // 2
X_ROWS = FIELDS + SHIFTS - 1
WIDE_RING = 8
PAIR_RING = 4
TOP1, TOP2, DENSE = 512, 256, 16
LAST = BLOCKS - 1


def pair_rows(c):
    return PAIR_ROWS if c else 2 * FIELDS


def build(nc, t):
    with ExitStack() as ctx:
        def sb(name, shape, dt=F32):
            return ctx.enter_context(nc.sbuf_tensor(name, shape, dt))

        def sem(name):
            return ctx.enter_context(nc.semaphore(name))

        ident = sb("ident", [P, P])
        ids = sb("ids_block", [P, FIELDS], U32)
        rows = sb("embedding_rows", [P, FIELDS * DIM])
        x_out = sb("x_out", [FIELDS, 2, TILE])
        x_base = sb("x_base", [PAIR_ROWS, TILE])
        x_pairs = sb("x_pairs", [PAIR_ROWS, PAIR_CHUNKS, TILE])
        x_wide = sb("x_wide", [P, 2, WIDE_CHUNKS, TILE])
        pair_z = sb("pair_products", [PAIR_ROWS, PAIR_RING, TILE])
        wide_z = sb("wide_products", [P, WIDE_RING, TILE])
        h1 = sb("h1_twice", [P, TILE])
        h2 = sb("h2_twice", [P, TILE])
        w0 = sb("w0", [PAIR_ROWS, PAIR_CHUNKS, P])
        w0_mirror = sb("w0_mirror", [PAIR_ROWS, PAIR_CHUNKS, P])
        w1 = sb("w1", [P, WIDE_CHUNKS, P])
        w2 = sb("w2", [P, WIDE_CHUNKS, P])
        b0 = sb("b0", [P, 1])
        b1 = sb("b1", [P, 1])
        b2 = sb("b2", [P, 1])
        wt1 = sb("wt1", [P, 2, TOP1])
        wt1_dense = sb("wt1_dense", [DENSE, TOP1])
        wt2 = sb("wt2", [P, TOP1 // P, TOP2])
        wt3 = sb("wt3", [P, TOP2 // P])
        bt1 = sb("bt1", [P, TOP1 // P])
        bt2 = sb("bt2", [P, TOP2 // P])
        direct01 = sb("direct01", [P, 2, TILE])
        direct2 = sb("direct2", [P, TILE])
        part01 = sb("part01", [P, TILES, P])
        part2 = sb("part2", [P, TILES, P])
        tower01 = sb("tower01", [P, BATCH])
        tower2 = sb("tower2", [P, BATCH])
        dense = x_pairs[0:DENSE, 0:BATCH // TILE, :].rearrange("p a n -> p (a n)")
        act1 = x_wide[:, 0, 0:2 * TOP1 // P, :].rearrange("p (s m) n -> p s m n", s=2)
        act2 = x_wide[:, 0, 8:8 + TOP2 // P, :]
        y_row = x_wide[0:1, 0, 12:16, :].rearrange("p a n -> p (a n)")

        bank = [ctx.enter_context(nc.psum_tensor(f"bank{i}", [P, TILE], F32)) for i in range(8)]
        acc0, acc1, acc2 = bank[0:3]
        x_bank = bank[3:5]
        top1_bank = bank[3:7]
        top2_bank = bank[0:2]
        y_bank = bank[7]

        x_rows = nc.dram_tensor("x_rows", [X_ROWS, COLS], F32, kind="Internal").ap()

        ident_zero = sem("ident_zero")
        ident_ready = sem("ident_ready")
        cin_weights = sem("cin_weights_loaded")
        top_weights = sem("top_weights_loaded")
        dense_loaded = sem("dense_loaded")
        w0_ready = sem("w0_ready")
        pad_ready = sem("pad_ready")
        ids_loaded = sem("ids_loaded")
        ids_in_place = sem("ids_in_place")
        x_bank_free = sem("x_bank_free")
        gathered = sem("rows_gathered")
        transposed = sem("x_transposed")
        x_copied = sem("x_copied")
        x_stored = [sem(f"x_stored{i}") for i in range(TILES)]
        pairs_loaded = sem("x_pairs_loaded")
        wide_loaded = [sem(f"x_wide_loaded{i}") for i in range(2)]
        pair_made = sem("pair_products_made")
        pair_used = sem("pair_products_used")
        wide_made = sem("wide_products_made")
        wide_used = sem("wide_products_used")
        out0 = sem("layer0_out")
        out1 = sem("layer1_out")
        out2 = sem("layer2_out")
        part01_made = sem("part01_made")
        part2_made = sem("part2_made")
        tower_made = sem("tower_made")
        top1_made = sem("top1_made")
        top1_out = sem("top1_out")
        top2_made = sem("top2_made")
        top2_out = sem("top2_out")
        y_made = sem("y_made")
        y_copied = sem("y_copied")
        y_stored = sem("y_stored")

        block = ctx.enter_context(nc.Block())

        def over_blocks(eng, body):
            body(0)
            with eng.Fori(1, LAST) as b:
                body(b)
            body(LAST)

        def last(b):
            return isinstance(b, int) and b == LAST

        def first(b):
            return isinstance(b, int) and b == 0

        def x_window(row, row_step, count, rows_in, col, lead=None):
            outer = [COLS, rows_in] if lead is None else [0, lead]
            return bass.AP(x_rows.tensor, row * COLS + col, [outer, [row_step * COLS, count], [1, TILE]])

        @block.gpsimd
        def _(pool):
            pool.memset(ident[:, :], 0.0).then_inc(ident_zero, 1)
            pool.wait_ge(ident_zero, 1)
            pool.affine_select(out=ident[:, :], in_=ident[:, :], compare_op=ALU.not_equal, fill=1.0,
                               base=0, pattern=[[-1, P]], channel_multiplier=1).then_inc(ident_ready, 1)

            def gather(b):
                if not first(b):
                    pool.wait_ge(gathered, b * (FIELDS * 16))
                pool.dma_start(ids[:, :], t["ids"][bass.ds(b * P, P), :]).then_inc(ids_loaded, 16)
                pool.wait_ge(ids_loaded, b * 16 + 16)
                if not first(b):
                    pool.wait_ge(transposed, b * TILES)
                pool.sem_inc(ids_in_place, 1)
                for f in range(FIELDS):
                    pool.indirect_dma_start(
                        out=rows[:, f * DIM:(f + 1) * DIM], out_offset=None, in_=t["tbl"][f],
                        in_offset=bass.IndirectOffsetOnAxis(ap=ids[:, f:f + 1], axis=0),
                    ).then_inc(gathered, 16)

            over_blocks(pool, gather)

        @block.sync
        def _(sp):
            sp.dma_start(w0[:, :, :], t["W0"].rearrange("c r s -> r c s")).then_inc(cin_weights, 16)
            sp.dma_start(w0_mirror[:, :, :], t["W0_mirror"].rearrange("c r s -> r c s")).then_inc(cin_weights, 16)
            full = (WIDE_CHUNKS - 1) * P
            for w, src in ((w1, t["W1"]), (w2, t["W2"])):
                sp.dma_start(w[:, 0:WIDE_CHUNKS - 1, :],
                             src[0:full, :].rearrange("(c r) s -> r c s", r=P)).then_inc(cin_weights, 16)
                sp.dma_start(w[0:HALF, WIDE_CHUNKS - 1, :], src[full:full + HALF, :]).then_inc(cin_weights, 16)
            for b, src in ((b0, t["b0"]), (b1, t["b1"]), (b2, t["b2"])):
                sp.dma_start(b[:, :], src.rearrange("(p o) -> p o", o=1)).then_inc(cin_weights, 16)

            def load_pairs(b, j, col):
                sp.wait_ge(x_stored[j], b * 32 + 32)
                for g in range(PAIR_GROUPS):
                    part = slice(g * FIELDS, (g + 1) * FIELDS)
                    sp.dma_start(x_base[part, :], x_rows[0:FIELDS, bass.ds(col, TILE)]).then_inc(pairs_loaded, 16)
                    c = 0 if g < 2 else 1
                    sp.dma_start(x_pairs[part, c:PAIR_CHUNKS, :],
                                 x_window(3 * c + 1 - g, 3, PAIR_CHUNKS - c, FIELDS, col)
                                 ).then_inc(pairs_loaded, 16)

            def load_wide(b, j, col):
                sp.wait_ge(x_stored[j], b * 32 + 32)
                for odd in range(2):
                    sp.dma_start(x_wide[odd * HALF:(odd + 1) * HALF, j % 2, :, :],
                                 x_window(odd, 2, WIDE_CHUNKS, 0, col, lead=HALF)
                                 ).then_inc(wide_loaded[j % 2], 16)

            load_pairs(0, 0, 0)
            load_wide(0, 0, 0)

            for w in range(2):
                sp.dma_start(wt1[:, w, :], t["Wt1"][w * P:(w + 1) * P, :]).then_inc(top_weights, 16)
            sp.dma_start(wt1_dense[:, :], t["Wt1"][2 * P:2 * P + DENSE, :]).then_inc(top_weights, 16)
            sp.dma_start(wt2[:, :, :], t["Wt2"].rearrange("(k r) s -> r k s", r=P)).then_inc(top_weights, 16)
            for dst, src in ((wt3, t["Wt3"].rearrange("(k r) o -> r (k o)", r=P)),
                             (bt1, t["bt1"].rearrange("(k r) -> r k", r=P)),
                             (bt2, t["bt2"].rearrange("(k r) -> r k", r=P))):
                with nc.allow_non_contiguous_dma(reason="a few hundred words, once"):
                    sp.dma_start(dst[:, :], src).then_inc(top_weights, 16)

            def loads(b):
                for j in range(TILES):
                    nb, nj = (b, j + 1) if j + 1 < TILES else (b + 1, 0)
                    if last(b) and j + 1 == TILES:
                        continue
                    col = b * (P * DIM) + (j + 1) * TILE
                    sp.wait_ge(pair_made, b * (TILES * PAIR_CHUNKS) + (j + 1) * PAIR_CHUNKS)
                    load_pairs(nb, nj, col)
                    if not (first(b) and j == 0):
                        sp.wait_ge(wide_made, b * (TILES * 2 * WIDE_CHUNKS) + j * 2 * WIDE_CHUNKS)
                    load_wide(nb, nj, col)

            over_blocks(sp, loads)
            sp.wait_ge(pair_made, BLOCKS * TILES * PAIR_CHUNKS)
            sp.dma_start(dense, t["dense"]).then_inc(dense_loaded, 16)
            sp.wait_ge(y_copied, BATCH // TILE)
            sp.dma_start(t["out"].rearrange("b o -> o b"), y_row).then_inc(y_stored, 16)
            sp.wait_ge(y_stored, 16)

        @block.vector
        def _(dve):
            nc.vector.memset(w1[HALF:P, WIDE_CHUNKS - 1, :], 0.0).then_inc(pad_ready, 1)
            nc.vector.memset(w2[HALF:P, WIDE_CHUNKS - 1, :], 0.0).then_inc(pad_ready, 1)
            dve.wait_ge(cin_weights, 16 * 9)
            nc.vector.tensor_tensor(w0[0:FIELDS, 0, :], w0[0:FIELDS, 0, :], w0_mirror[0:FIELDS, 0, :], ALU.add)
            nc.vector.tensor_tensor(w0[:, 1:PAIR_CHUNKS, :], w0[:, 1:PAIR_CHUNKS, :],
                                    w0_mirror[:, 1:PAIR_CHUNKS, :], ALU.add).then_inc(w0_ready, 1)

            def pair_products(b, j):
                base = b * (TILES * PAIR_CHUNKS) + j * PAIR_CHUNKS
                dve.wait_ge(pairs_loaded, b * (TILES * 96) + (j + 1) * 96)
                for c in range(PAIR_CHUNKS):
                    n = j * PAIR_CHUNKS + c
                    if not (first(b) and n < PAIR_RING):
                        dve.wait_ge(pair_used, base + c + 1 - PAIR_RING)
                    r = pair_rows(c)
                    nc.vector.tensor_tensor(pair_z[0:r, n % PAIR_RING, :], x_base[0:r, :], x_pairs[0:r, c, :],
                                            ALU.mult).then_inc(pair_made, 1)

            def wide_products(b, j, layer, h):
                for c in range(WIDE_CHUNKS):
                    n = (2 * j + layer - 1) * WIDE_CHUNKS + c
                    if not (first(b) and n < WIDE_RING):
                        dve.wait_ge(wide_used, b * (TILES * 2 * WIDE_CHUNKS) + n + 1 - WIDE_RING)
                    nc.vector.tensor_tensor(wide_z[:, n % WIDE_RING, :], x_wide[:, j % 2, c, :], h[:, :],
                                            ALU.mult).then_inc(wide_made, 1)

            def sum_layer2(b, j):
                dve.wait_ge(out2, b * TILES + j + 1)
                nc.vector.tensor_reduce(part2[:, j % TILES, :], direct2[:, :].rearrange("p (d b) -> p b d", b=P),
                                        AX.X, ALU.add).then_inc(part2_made, 1)
                if j % TILES == TILES - 1:
                    dve.wait_ge(part2_made, b * TILES + j + 1)
                    at = b * P if j > 0 else b * P - P
                    nc.vector.tensor_reduce(tower2[:, bass.ds(at, P)], part2[:, :, :].rearrange("p j b -> p b j"),
                                            AX.X, ALU.add).then_inc(tower_made, 1)

            pair_products(0, 0)

            def body(b):
                for j in range(TILES):
                    t3 = b * (3 * TILES) + 3 * j
                    dve.wait_ge(out0, t3 + 2)
                    dve.wait_ge(wide_loaded[j % 2], b * (TILES * 16) + (j // 2 + 1) * 32)
                    wide_products(b, j, 1, h1)
                    if not (last(b) and j + 1 == TILES):
                        pair_products(b, j + 1)
                    if not (first(b) and j == 0):
                        sum_layer2(b, j - 1)
                    dve.wait_ge(out1, t3 + 2)
                    wide_products(b, j, 2, h2)
                    dve.wait_ge(out0, t3 + 3)
                    dve.wait_ge(out1, t3 + 3)
                    nc.vector.tensor_reduce(part01[:, j, :],
                                            direct01[:, j % 2, :].rearrange("p (d b) -> p b d", b=P),
                                            AX.X, ALU.add).then_inc(part01_made, 1)
                dve.wait_ge(part01_made, b * TILES + TILES)
                nc.vector.tensor_reduce(tower01[:, bass.ds(b * P, P)], part01[:, :, :].rearrange("p j b -> p b j"),
                                        AX.X, ALU.add).then_inc(tower_made, 1)

            over_blocks(dve, body)
            sum_layer2(LAST, TILES - 1)

        @block.tensor
        def _(pe):
            def transposes(b, j):
                n = b * TILES + j
                if not (first(b) and j < 2):
                    pe.wait_ge(x_copied, n - 1)
                    pe.sem_inc(x_bank_free, 1)
                bank_ = x_bank[j % 2]
                by_d = rows[:, :].rearrange("p (f d) -> p d f", d=DIM)
                for k in range(D_PER_TILE):
                    ins = nc.tensor.transpose(bank_[0:FIELDS, k * P:(k + 1) * P],
                                              by_d[:, j * D_PER_TILE + k, :], ident[:, :])
                ins.then_inc(transposed, 1)

            def layer0(b, j):
                base = b * (TILES * PAIR_CHUNKS) + j * PAIR_CHUNKS
                if not (first(b) and j == 0):
                    pe.wait_ge(out0, b * (3 * TILES) + 3 * j)
                for c in range(PAIR_CHUNKS):
                    r = pair_rows(c)
                    pe.wait_ge(pair_made, base + c + 1)
                    nc.tensor.matmul(acc0[:, :], w0[0:r, c, :], pair_z[0:r, (j * PAIR_CHUNKS + c) % PAIR_RING, :],
                                     start=(c == 0), stop=(c == PAIR_CHUNKS - 1)).then_inc(pair_used, 1)

            def wide_layer(b, j, layer, w, acc):
                for c in range(WIDE_CHUNKS):
                    n = (2 * j + layer - 1) * WIDE_CHUNKS + c
                    pe.wait_ge(wide_made, b * (TILES * 2 * WIDE_CHUNKS) + n + 1)
                    nc.tensor.matmul(acc[:, :], w[:, c, :], wide_z[:, n % WIDE_RING, :],
                                     start=(c == 0), stop=(c == WIDE_CHUNKS - 1)).then_inc(wide_used, 1)

            pe.wait_ge(ident_ready, 1)
            pe.wait_ge(gathered, FIELDS * 16)
            for j in range(TILES):
                transposes(0, j)
            pe.wait_ge(w0_ready, 1)
            layer0(0, 0)
            pe.wait_ge(pad_ready, 2)

            def body(b):
                for j in range(TILES):
                    if j == TILES // 2 and not last(b):
                        pe.wait_ge(gathered, b * (FIELDS * 16) + 2 * FIELDS * 16)
                    if j >= TILES // 2 and not last(b):
                        transposes(b + 1, 2 * j - TILES)
                        transposes(b + 1, 2 * j - TILES + 1)
                    if not (first(b) and j == 0):
                        pe.wait_ge(out1, b * (3 * TILES) + 3 * j)
                    wide_layer(b, j, 1, w1, acc1)
                    if not (last(b) and j + 1 == TILES):
                        layer0(b, j + 1)
                    if not (first(b) and j == 0):
                        pe.wait_ge(out2, b * TILES + j)
                    wide_layer(b, j, 2, w2, acc2)

            over_blocks(pe, body)

            def top_layer1(q):
                if q:
                    pe.wait_ge(top1_out, 4 * q)
                for m in range(TOP1 // P):
                    for k, (w, x) in enumerate(((wt1[:, 0, :], tower01), (wt1[:, 1, :], tower2),
                                                (wt1_dense[:, :], dense))):
                        ins = nc.tensor.matmul(top1_bank[m][:, :], w[:, m * P:(m + 1) * P],
                                               x[:, q * TILE:(q + 1) * TILE], start=(k == 0), stop=(k == 2))
                    ins.then_inc(top1_made, 1)

            def top_layers23(q):
                pe.wait_ge(top1_out, 4 * q + 4)
                if q:
                    pe.wait_ge(top2_out, 2 * q)
                for m in range(TOP2 // P):
                    for k in range(TOP1 // P):
                        ins = nc.tensor.matmul(top2_bank[m][:, :], wt2[:, k, m * P:(m + 1) * P],
                                               act1[:, q % 2, k, :], start=(k == 0), stop=(k == TOP1 // P - 1))
                    ins.then_inc(top2_made, 1)
                pe.wait_ge(top2_out, 2 * q + 2)
                if q:
                    pe.wait_ge(y_copied, q)
                for k in range(TOP2 // P):
                    ins = nc.tensor.matmul(y_bank[0:1, :], wt3[:, k:k + 1], act2[:, k, :],
                                           start=(k == 0), stop=(k == TOP2 // P - 1))
                ins.then_inc(y_made, 1)

            pe.wait_ge(top_weights, 16 * 7)
            pe.wait_ge(dense_loaded, 16)
            pe.wait_ge(tower_made, 2 * BLOCKS)
            pe.wait_ge(x_copied, BLOCKS * TILES)
            groups = BATCH // TILE
            top_layer1(0)
            for q in range(groups):
                if q + 1 < groups:
                    top_layer1(q + 1)
                top_layers23(q)

        @block.scalar
        def _(act):
            act.wait_ge(cin_weights, 16 * 9)

            def store_x(b, j):
                n = b * TILES + j
                act.wait_ge(transposed, n + 1)
                if j >= 2:
                    act.wait_ge(x_stored[j - 2], b * 32 + 32)
                elif not first(b):
                    act.wait_ge(x_stored[j + 2], b * 32)
                nc.scalar.activation(x_out[:, j % 2, :], x_bank[j % 2][0:FIELDS, :], ACT.Copy).then_inc(x_copied, 1)
                act.wait_ge(x_copied, n + 1)
                col = b * (P * DIM) + j * TILE
                act.dma_start(x_rows[0:FIELDS, bass.ds(col, TILE)], x_out[:, j % 2, :]).then_inc(x_stored[j], 16)
                act.dma_start(x_rows[FIELDS:X_ROWS, bass.ds(col, TILE)],
                              x_out[0:X_ROWS - FIELDS, j % 2, :]).then_inc(x_stored[j], 16)

            def finish_layer(acc, bias, h, direct, done):
                low, high = slice(0, HALF), slice(HALF, P)
                nc.scalar.activation(h[low, :], acc[low, :], ACT.Relu, bias=bias[low, :]).then_inc(done, 1)
                nc.scalar.activation(h[high, :], acc[low, :], ACT.Relu, bias=bias[low, :]).then_inc(done, 1)
                nc.scalar.activation(direct, acc[high, :], ACT.Relu, bias=bias[high, :]).then_inc(done, 1)

            def finish0(b, j):
                act.wait_ge(pair_used, b * (TILES * PAIR_CHUNKS) + (j + 1) * PAIR_CHUNKS)
                if not (first(b) and j < 2):
                    act.wait_ge(part01_made, b * TILES + j - 1)
                finish_layer(acc0, b0, h1, direct01[0:HALF, j % 2, :], out0)

            for j in range(TILES):
                store_x(0, j)
            finish0(0, 0)

            def body(b):
                for j in range(TILES):
                    if j >= TILES // 2 and not last(b):
                        store_x(b + 1, 2 * j - TILES)
                        store_x(b + 1, 2 * j - TILES + 1)
                    done = b * (TILES * 2 * WIDE_CHUNKS) + 2 * j * WIDE_CHUNKS
                    act.wait_ge(wide_used, done + WIDE_CHUNKS)
                    finish_layer(acc1, b1, h2, direct01[HALF:P, j % 2, :], out1)
                    if not (last(b) and j + 1 == TILES):
                        finish0(b, j + 1)
                    act.wait_ge(wide_used, done + 2 * WIDE_CHUNKS)
                    if not (first(b) and j == 0):
                        act.wait_ge(part2_made, b * TILES + j)
                    nc.scalar.activation(direct2[:, :], acc2[:, :], ACT.Relu, bias=b2[:, :]).then_inc(out2, 1)

            over_blocks(act, body)

            def finish_top1(q):
                for m in range(TOP1 // P):
                    act.wait_ge(top1_made, 4 * q + m + 1)
                    if q >= 2 and m == 0:
                        act.wait_ge(top2_made, 2 * (q - 1))
                    nc.scalar.activation(act1[:, q % 2, m, :], top1_bank[m][:, :], ACT.Relu,
                                         bias=bt1[:, m:m + 1]).then_inc(top1_out, 1)

            groups = BATCH // TILE
            act.wait_ge(top_weights, 16 * 7)
            finish_top1(0)
            for q in range(groups):
                if q + 1 < groups:
                    finish_top1(q + 1)
                for m in range(TOP2 // P):
                    act.wait_ge(top2_made, 2 * q + m + 1)
                    if q and m == 0:
                        act.wait_ge(y_made, q)
                    nc.scalar.activation(act2[:, m, :], top2_bank[m][:, :], ACT.Relu,
                                         bias=bt2[:, m:m + 1]).then_inc(top2_out, 1)
                act.wait_ge(y_made, q + 1)
                nc.scalar.activation(y_row[:, q * TILE:(q + 1) * TILE], y_bank[0:1, :], ACT.Copy).then_inc(y_copied, 1)


def kernel(**inputs):
    import numpy as np
    import concourse.bacc as bacc
    from concourse.bass_utils import run_bass_kernel_spmd

    given = {k: np.ascontiguousarray(v) for k, v in inputs.items()}
    c, g, f = np.meshgrid(np.arange(PAIR_CHUNKS), np.arange(PAIR_GROUPS), np.arange(FIELDS), indexing="ij")
    partner = (f + 3 * c + 1 - g) % FIELDS
    shape = (PAIR_CHUNKS, PAIR_ROWS, P)
    W0 = given["L0_rec_W0"]
    arrays = {
        "ids": given["ids"],
        "dense": np.ascontiguousarray(given["dense_ctx"].T),
        "W0": W0[(f * FIELDS + partner).ravel()].reshape(shape),
        "W0_mirror": W0[(partner * FIELDS + f).ravel()].reshape(shape),
        "W1": given["L0_rec_W1"], "W2": given["L0_rec_W2"],
        "b0": given["L0_rec_b0"], "b1": given["L0_rec_b1"], "b2": given["L0_rec_b2"],
        "Wt1": given["W_top1"], "bt1": given["b_top1"], "Wt2": given["W_top2"], "bt2": given["b_top2"],
        "Wt3": given["W_top3"],
    }
    for i in range(FIELDS):
        arrays[f"tbl_{i}"] = given[f"tbl_{i}"]

    nc = bacc.Bacc("TRN2", target_bir_lowering=False, num_devices=1)
    t = {n: nc.dram_tensor(f"in_{n}", a.shape, mybir.dt.from_np(a.dtype), kind="ExternalInput").ap()
         for n, a in arrays.items()}
    t["ids"] = t["ids"].bitcast(U32)
    t["tbl"] = [t[f"tbl_{i}"] for i in range(FIELDS)]
    t["out"] = nc.dram_tensor("out_y", (BATCH, 1), F32, kind="ExternalOutput").ap()
    build(nc, t)
    r = run_bass_kernel_spmd(nc, [{f"in_{n}": a for n, a in arrays.items()}], core_ids=[0])
    return r.results[0]["out_y"]
```

```python
from contextlib import ExitStack

import concourse.bass as bass
from concourse import mybir

F32 = mybir.dt.float32
F32R = mybir.dt.float32r
U32 = mybir.dt.uint32
ALU = mybir.AluOpType
ACT = mybir.ActivationFunctionType
AX = mybir.AxisListType

FIELDS, DIM, BATCH = 39, 16, 2048
P = 128
HALF = 64
TILE = 512
BLOCKS = BATCH // P
D_PER_TILE = TILE // P
TILES = DIM // D_PER_TILE
COLS = BATCH * DIM
SHIFTS = FIELDS // 2 + 1
PAIR_CHUNKS = 7
PAIR_GROUPS = 3
PAIR_ROWS = PAIR_GROUPS * FIELDS
WIDE_CHUNKS = (FIELDS + 1) // 2
X_ROWS = FIELDS + PAIR_GROUPS * PAIR_CHUNKS - 1
CHUNKS = (PAIR_CHUNKS, WIDE_CHUNKS, WIDE_CHUNKS)
PLAN = (
    ((3, "full"), (2, "pool"), (2, "own")),
    ((2, "full"), (2, "pool"), (2, "own"), (2, "pool"), (3, "full"), (2, "pool"), (2, "own"),
     (2, "pool"), (3, "full")),
    ((3, "full"), (2, "pool"), (2, "own"), (2, "pool"), (2, "full"), (2, "pool"), (2, "own"),
     (2, "pool"), (3, "full")),
)
SPLIT_KINDS = ("pool", "own")
FULL_UNIT, SPLIT_UNIT = 3, 2
FULL_RING = 2
Z_RING = {"pool": 2, "own": 1}
HI_RING = {"pool": 3, "own": 1}
LO_RING = {"pool": 2, "own": 1}
TOP1, TOP2, DENSE = 512, 256, 16
GROUPS = BATCH // TILE
LAST = BLOCKS - 1
FINISH2_AT, FINISH0_AT, COPY_X_AT = 3, 3, 4
GATHERS = {2: (0, 1, 0, 3, 2, 0, 1, 0, 3), 3: (0, 1, 0, 3, 2, 0, 2, 0, 3),
           0: (0, 1, 0, 3, 2, 0, 2, 0, 3), 1: (0, 1, 0, 3, 3, 0, 0, 0, 0)}
AHEAD_GATHERS = sum(GATHERS[2]) + sum(GATHERS[3])
FIRST_GATHERS = 15


def pair_rows(c):
    return PAIR_ROWS if c < PAIR_CHUNKS - 1 else 2 * FIELDS


def shift(c, g):
    return 3 * c + (1, 0, 2)[g]


def units(layer):
    ends = [sum(n for n, _ in PLAN[layer][:u + 1]) for u in range(len(PLAN[layer]))]
    return [(u, end - PLAN[layer][u][0], end) for u, end in enumerate(ends)]


def kind_of(layer, u):
    return PLAN[layer][u][1]


def count(kind, order):
    return sum(kind_of(l, u) == kind for l, u in order)


def split_units(layer):
    return [u for u, _, _ in units(layer) if kind_of(layer, u) != "full"]


def weight_slot(layer, c):
    kinds = [kind_of(layer, u) == "full" for u, c0, c1 in units(layer) for _ in range(c0, c1)]
    return kinds[:c].count(kinds[c])


ORDER = [(l, u) for l in (1, 0, 2) for u, _, _ in units(l)]
ORDER0 = [(0, u) for u, _, _ in units(0)]
SPLIT_CHUNKS = [sum(c1 - c0 for u, c0, c1 in units(l) if kind_of(l, u) != "full") for l in range(3)]
FIRST_PAIRS = units(0)[0][2]
FIRST_WIDE = [c1 for _, _, c1 in units(1) if 2 * c1 >= WIDE_CHUNKS][0]
assert [units(l)[-1][2] for l in range(3)] == list(CHUNKS)
assert TILES * count("full", ORDER) % FULL_RING == 0
assert all(TILES * count(k, ORDER) % ring[k] == 0 for k in SPLIT_KINDS for ring in (Z_RING, HI_RING, LO_RING))
assert sum(map(sum, GATHERS.values())) == FIELDS
assert len(split_units(1)) > max(FINISH2_AT, COPY_X_AT) and len(split_units(2)) > FINISH0_AT


def build(nc, t):
    with ExitStack() as ctx:
        def sb(name, shape, dt=F32):
            return ctx.enter_context(nc.sbuf_tensor(name, shape, dt))

        def sem(name):
            return ctx.enter_context(nc.semaphore(name))

        ident = sb("ident", [P, P])
        ids_all = sb("ids_all", [P, BLOCKS, FIELDS], U32)
        ids = sb("ids_block", [P, FIELDS], U32)
        rows_in = sb("rows_in", [P, FIELDS * DIM])
        rows = sb("embedding_rows", [P, FIELDS * DIM])
        x_out = sb("x_out", [FIELDS, 2, TILE])
        x_base = sb("x_base", [PAIR_ROWS, TILE])
        x_pairs = sb("x_pairs", [PAIR_ROWS, PAIR_CHUNKS, TILE])
        x_wide = sb("x_wide", [P, 2, WIDE_CHUNKS, TILE])
        z_full = sb("z_full", [P, FULL_RING, FULL_UNIT, TILE])
        z_split = {k: sb(f"z_{k}", [P, Z_RING[k], SPLIT_UNIT, TILE]) for k in SPLIT_KINDS}
        z_hi = {k: sb(f"z_hi_{k}", [P, HI_RING[k], SPLIT_UNIT, TILE], F32R) for k in SPLIT_KINDS}
        z_lo = {k: sb(f"z_lo_{k}", [P, LO_RING[k], SPLIT_UNIT, TILE], F32R) for k in SPLIT_KINDS}
        w_full = [sb(f"w{l}_full", [P, CHUNKS[l] - SPLIT_CHUNKS[l], P]) for l in range(3)]
        w_hi = [sb(f"w{l}_hi", [P, SPLIT_CHUNKS[l], P], F32R) for l in range(3)]
        w_lo = [sb(f"w{l}_lo", [P, SPLIT_CHUNKS[l], P], F32R) for l in range(3)]
        b0 = sb("b0", [P, 1])
        b1 = sb("b1", [P, 1])
        b2 = sb("b2", [P, 1])
        bt1 = sb("bt1", [P, TOP1 // P])
        bt2 = sb("bt2", [P, TOP2 // P])
        wt3 = sb("wt3", [P, TOP2 // P])
        direct01 = sb("direct01", [P, 2, TILE])
        direct2 = sb("direct2", [P, TILE])
        part = sb("part", [P, 2, P])
        block_sum = sb("block_sum", [P, 2, P])
        tower_out = sb("tower_out", [P, 2, P])

        stage = x_wide[:, 1, :, :].rearrange("p c n -> p (c n)")
        at = 0
        w_raw = []
        for l in range(3):
            w_raw.append(stage[:, at:at + CHUNKS[l] * P].rearrange("p (c s) -> p c s", s=P))
            at += CHUNKS[l] * P
        w0_mirror = stage[:, at:at + PAIR_CHUNKS * P].rearrange("p (c s) -> p c s", s=P)

        late = x_pairs[:, :, :].rearrange("p c n -> p (c n)")
        wt1_dense = late[0:DENSE, 0:TOP1]
        free = x_wide[:, 0, :, :].rearrange("p c n -> p (c n)")
        wt1 = free[:, 0:2 * TOP1].rearrange("p (k s) -> p k s", k=2)
        wt2 = free[:, 2 * TOP1:4 * TOP1].rearrange("p (k s) -> p k s", k=TOP1 // P)
        dense = late[0:DENSE, TOP1:TOP1 + BATCH]
        tower = x_wide[:, 0, 4:4 + 2 * BATCH // TILE, :].rearrange("p c n -> p (c n)").rearrange(
            "p (k n) -> p k n", k=2)
        act1 = x_wide[:, 0, 12:12 + TOP1 // P, :]
        act2 = x_wide[:, 0, 16:16 + TOP2 // P, :]
        y_row = x_wide[0:1, 1, 0:GROUPS, :].rearrange("p a n -> p (a n)")

        bank = [ctx.enter_context(nc.psum_tensor(f"bank{i}", [P, TILE], F32)) for i in range(8)]
        acc0, acc1, acc2 = bank[0:3]
        x_bank = bank[3:5]
        h1, h2, x_again = bank[5:8]
        top1_bank = bank[3:6] + bank[7:8]
        top2_bank = bank[0:2]
        y_bank = bank[6]

        x_rows = nc.dram_tensor("x_rows", [X_ROWS, COLS], F32, kind="Internal").ap()
        tower_rows = nc.dram_tensor("tower_rows", [P, 2, BATCH], F32, kind="Internal").ap()

        ident_zero = sem("ident_zero")
        ident_ready = sem("ident_ready")
        cin_weights = sem("cin_weights_loaded")
        top_weights = sem("top_weights_loaded")
        biases_loaded = sem("biases_loaded")
        pad_zero = sem("pad_zero")
        w0_added = sem("w0_added")
        w_hi_made = sem("w_hi_made")
        weights_ready = sem("weights_ready")
        ids_loaded = sem("ids_loaded")
        ids_copied = sem("ids_copied")
        gather_may_start = sem("gather_may_start")
        rows_moved = sem("rows_moved")
        x_bank_free = sem("x_bank_free")
        gathered = sem("rows_gathered")
        transposed = sem("x_transposed")
        x_copied = sem("x_copied")
        x_stored = [sem(f"x_stored{i}") for i in range(TILES)]
        pairs_loaded = sem("x_pairs_loaded")
        first_pairs_loaded = sem("first_pairs_loaded")
        first_wide_loaded = sem("first_wide_loaded")
        wide_loaded = [sem(f"x_wide_loaded{i}") for i in range(2)]
        made = {k: sem(f"{k}_products_made") for k in ("full", "pool", "own")}
        used = {k: sem(f"{k}_products_used") for k in ("full", "pool", "own")}
        hi_made = {k: sem(f"{k}_hi_made") for k in SPLIT_KINDS}
        lo_made = {k: sem(f"{k}_lo_made") for k in SPLIT_KINDS}
        x_again_made = sem("x_again_made")
        out0 = sem("layer0_out")
        out1 = sem("layer1_out")
        out2 = sem("layer2_out")
        sums = [sem(f"tower_sums{k}") for k in range(2)]
        tower_stored = [sem(f"tower_stored{k}") for k in range(2)]
        tower_loaded = sem("tower_loaded")
        top1_made = sem("top1_made")
        top1_out = sem("top1_out")
        top2_made = sem("top2_made")
        top2_out = sem("top2_out")
        y_made = sem("y_made")
        y_copied = sem("y_copied")
        y_stored = sem("y_stored")

        block = ctx.enter_context(nc.Block())

        def over_blocks(eng, body):
            body(0)
            with eng.Fori(1, LAST) as b:
                body(b)
            body(LAST)

        def last(b):
            return isinstance(b, int) and b == LAST

        def first(b):
            return isinstance(b, int) and b == 0

        def x_window(row, row_step, count, rows_in, col, lead=None):
            outer = [COLS, rows_in] if lead is None else [0, lead]
            return bass.AP(x_rows.tensor, row * COLS + col, [outer, [row_step * COLS, count], [1, TILE]])

        def unit_no(b, j, layer, u):
            kind = kind_of(layer, u)
            if layer == 0:
                if first(b) and j == 0:
                    return count(kind, ORDER0[:u])
                j = j - 1
            n = count(kind, ORDER0) + j * count(kind, ORDER) + count(kind, ORDER[:ORDER.index((layer, u))])
            if last(b) and j == TILES - 1 and layer == 2:
                n -= count(kind, ORDER0)
            return n if first(b) else b * (TILES * count(kind, ORDER)) + n

        def slot(b, j, layer, u, ring):
            return unit_no(b if isinstance(b, int) else 1, j, layer, u) % ring

        def wait_slot_free(eng, sem_, b, n, ring):
            if not (first(b) and n < ring):
                eng.wait_ge(sem_, n + 1 - ring)

        def wait_z_made(eng, b, j, layer):
            u = units(layer)[-1][0]
            eng.wait_ge(made[kind_of(layer, u)], unit_no(b, j, layer, u) + 1)

        def wait_accumulated(eng, b, j, layer):
            u = units(layer)[-1][0]
            if kind_of(layer, u) == "full" and kind_of(layer, u - 1) != "full":
                u -= 1
            eng.wait_ge(used[kind_of(layer, u)], unit_no(b, j, layer, u) + 1)

        def make_lo(eng, b, j, layer, u):
            kind, (_, c0, c1), r = kind_of(layer, u), units(layer)[u], slice(0, P if layer else PAIR_ROWS)
            n, m = unit_no(b, j, layer, u), slice(0, c1 - c0)
            eng.wait_ge(hi_made[kind], n + 1)
            wait_slot_free(eng, used[kind], b, n, LO_RING[kind])
            eng.tensor_tensor(z_lo[kind][r, slot(b, j, layer, u, LO_RING[kind]), m, :],
                              z_split[kind][r, slot(b, j, layer, u, Z_RING[kind]), m, :],
                              z_hi[kind][r, slot(b, j, layer, u, HI_RING[kind]), m, :].bitcast(F32),
                              ALU.subtract).then_inc(lo_made[kind], 1)

        @block.gpsimd
        def _(pool):
            pool.memset(ident[:, :], 0.0).then_inc(ident_zero, 1)
            pool.wait_ge(ident_zero, 1)
            pool.affine_select(out=ident[:, :], in_=ident[:, :], compare_op=ALU.not_equal, fill=1.0,
                               base=0, pattern=[[-1, P]], channel_multiplier=1).then_inc(ident_ready, 1)

            def start_block(b):
                if not first(b):
                    pool.wait_ge(gathered, b * (FIELDS * 16))
                    pool.wait_ge(rows_moved, b)
                pool.sem_inc(gather_may_start, 1)
                nc.gpsimd.tensor_copy(ids[:, :], ids_all[:, bass.ds(b, 1), :].rearrange("p o f -> p (o f)")
                                      ).then_inc(ids_copied, 1)
                pool.wait_ge(ids_copied, b + 1)
                pool.sem_inc(gather_may_start, 1)

            def gather(b, fields):
                for f in fields:
                    pool.indirect_dma_start(
                        out=rows_in[:, f * DIM:(f + 1) * DIM], out_offset=None, in_=t["tbl"][f],
                        in_offset=bass.IndirectOffsetOnAxis(ap=ids[:, f:f + 1], axis=0),
                    ).then_inc(gathered, 16)

            pool.dma_start(ids_all[:, :, :], t["ids"].rearrange("(b p) f -> p b f", p=P)).then_inc(ids_loaded, 16)
            pool.wait_ge(ids_loaded, 16)
            start_block(0)
            gather(0, range(FIELDS))
            start_block(1)
            gather(1, range(FIRST_GATHERS))
            for l, u in ORDER0:
                if kind_of(l, u) == "pool":
                    make_lo(pool, 0, 0, 0, u)
            gather(1, range(FIRST_GATHERS, AHEAD_GATHERS))

            def body(b):
                for j in range(TILES):
                    ending = isinstance(b, int) and b >= LAST - 1
                    los = [(l, u) for l, u in ORDER if kind_of(l, u) == "pool"
                           and not (l == 0 and last(b) and j == TILES - 1)]
                    due = not (j >= TILES // 2 and ending or last(b))
                    done = {2: 0, 3: sum(GATHERS[2]), 0: AHEAD_GATHERS, 1: FIELDS - sum(GATHERS[1])}[j]
                    for i, (layer, u) in enumerate(los):
                        make_lo(pool, b, j + (layer == 0), layer, u)
                        if due and GATHERS[j][i]:
                            if j == TILES // 2 and not any(GATHERS[j][:i]):
                                start_block(b + 2)
                            gather(b + 2 if j >= TILES // 2 else b + 1, range(done, done + GATHERS[j][i]))
                            done += GATHERS[j][i]

            body(0)
            with pool.Fori(1, LAST - 1) as b:
                body(b)
            body(LAST - 1)
            body(LAST)

        @block.sync
        def _(sp):
            sp.wait_ge(pad_zero, 1)
            sp.dma_start(w_raw[0][0:PAIR_ROWS, :, :], t["W0"].rearrange("c r s -> r c s")).then_inc(cin_weights, 16)
            mirror = t["W0_mirror"].rearrange("c r s -> r c s")
            for g in (0, 2):
                part = slice(g * FIELDS, (g + 1) * FIELDS)
                sp.dma_start(w0_mirror[part, 0, :], mirror[part, 0, :]).then_inc(cin_weights, 16)
            sp.dma_start(w0_mirror[0:PAIR_ROWS, 1:PAIR_CHUNKS, :],
                         mirror[:, 1:PAIR_CHUNKS, :]).then_inc(cin_weights, 16)
            full = (WIDE_CHUNKS - 1) * P
            for w, src in ((w_raw[1], t["W1"]), (w_raw[2], t["W2"])):
                sp.dma_start(w[:, 0:WIDE_CHUNKS - 1, :],
                             src[0:full, :].rearrange("(c r) s -> r c s", r=P)).then_inc(cin_weights, 16)
                sp.dma_start(w[0:HALF, WIDE_CHUNKS - 1, :], src[full:full + HALF, :]).then_inc(cin_weights, 16)
            for b, src in ((b0, t["b0"]), (b1, t["b1"]), (b2, t["b2"])):
                sp.dma_start(b[:, :], src.rearrange("(p o) -> p o", o=1)).then_inc(biases_loaded, 16)
            with nc.allow_non_contiguous_dma(reason="a few hundred words, once"):
                for dst, src in ((wt3, t["Wt3"].rearrange("(k r) o -> r (k o)", r=P)),
                                 (bt1, t["bt1"].rearrange("(k r) -> r k", r=P)),
                                 (bt2, t["bt2"].rearrange("(k r) -> r k", r=P))):
                    sp.dma_start(dst[:, :], src).then_inc(biases_loaded, 16)

            def load_first_pairs():
                sp.wait_ge(x_stored[0], 32)
                cuts = (0, FIRST_PAIRS, FIRST_PAIRS + 2, PAIR_CHUNKS)
                for i, (c0, c1) in enumerate(zip(cuts, cuts[1:])):
                    for g in range(PAIR_GROUPS):
                        part = slice(g * FIELDS, (g + 1) * FIELDS)
                        if i == 0:
                            sp.dma_start(x_base[part, :], x_rows[0:FIELDS, 0:TILE]).then_inc(first_pairs_loaded, 16)
                        sp.dma_start(x_pairs[part, c0:c1, :], x_window(shift(c0, g), 3, c1 - c0, FIELDS, 0)
                                     ).then_inc(pairs_loaded if i else first_pairs_loaded, 16)

            def load_pairs(b, j, col):
                sp.wait_ge(x_stored[j], b * 32 + 32)
                for g in range(PAIR_GROUPS):
                    part = slice(g * FIELDS, (g + 1) * FIELDS)
                    sp.dma_start(x_base[part, :], x_rows[0:FIELDS, bass.ds(col, TILE)]).then_inc(pairs_loaded, 16)
                    sp.dma_start(x_pairs[part, :, :], x_window(shift(0, g), 3, PAIR_CHUNKS, FIELDS, col)
                                 ).then_inc(pairs_loaded, 16)

            def load_wide(b, j, col, c0=0, c1=WIDE_CHUNKS, done=None):
                sp.wait_ge(x_stored[j], b * 32 + 32)
                for odd in range(2):
                    sp.dma_start(x_wide[odd * HALF:(odd + 1) * HALF, j % 2, c0:c1, :],
                                 x_window(2 * c0 + odd, 2, c1 - c0, 0, col, lead=HALF)
                                 ).then_inc(done or wide_loaded[j % 2], 16)

            def store_x(b, j):
                sp.wait_ge(x_copied, b * TILES + j + 1)
                col = b * (P * DIM) + j * TILE
                sp.dma_start(x_rows[0:FIELDS, bass.ds(col, TILE)], x_out[:, j % 2, :]).then_inc(x_stored[j], 16)
                sp.dma_start(x_rows[FIELDS:X_ROWS, bass.ds(col, TILE)],
                             x_out[0:X_ROWS - FIELDS, j % 2, :]).then_inc(x_stored[j], 16)

            store_x(0, 0)
            store_x(0, 1)
            load_first_pairs()
            store_x(0, 2)
            store_x(0, 3)
            load_wide(0, 0, 0, 0, FIRST_WIDE, first_wide_loaded)

            def loads(b):
                for j in range(TILES):
                    if j == 1 and not first(b):
                        for k in range(2):
                            sp.wait_ge(sums[k], b * (2 * TILES - 1))
                            sp.dma_start(tower_rows[:, k, bass.ds((b - 1) * P, P)],
                                         tower_out[:, k, :]).then_inc(tower_stored[k], 16)
                    nb, nj = (b, j + 1) if j + 1 < TILES else (b + 1, 0)
                    if last(b) and j + 1 == TILES:
                        continue
                    col = b * (P * DIM) + (j + 1) * TILE
                    if j + 1 == TILES:
                        store_x(b + 1, 0)
                        store_x(b + 1, 1)
                    if j == 0 and not first(b):
                        store_x(b, 2)
                        store_x(b, 3)
                    wait_z_made(sp, b, j, 0)
                    load_pairs(nb, nj, col)
                    if first(b) and j == 0:
                        load_wide(0, 0, 0, FIRST_WIDE, WIDE_CHUNKS)
                    if j:
                        wait_z_made(sp, b, j - 1, 2)
                    elif not first(b):
                        wait_z_made(sp, b - 1, TILES - 1, 2)
                    else:
                        sp.wait_ge(weights_ready, 1)
                    load_wide(nb, nj, col)

            over_blocks(sp, loads)
            wait_z_made(sp, LAST, TILES - 1, 0)
            sp.dma_start(dense, t["dense"]).then_inc(top_weights, 16)
            sp.dma_start(wt1_dense, t["Wt1"][2 * P:2 * P + DENSE, :]).then_inc(top_weights, 16)
            wait_z_made(sp, LAST, TILES - 2, 2)
            sp.dma_start(wt1, t["Wt1"][0:2 * P, :].rearrange("(k r) s -> r k s", r=P)).then_inc(top_weights, 16)
            sp.dma_start(wt2, t["Wt2"].rearrange("(k r) s -> r k s", r=P)).then_inc(top_weights, 16)
            for k in range(2):
                sp.wait_ge(tower_stored[k], LAST * 16)
                sp.dma_start(tower[:, k, 0:LAST * P], tower_rows[:, k, 0:LAST * P]).then_inc(tower_loaded, 16)
            sp.wait_ge(y_copied, GROUPS)
            sp.dma_start(t["out"].rearrange("b o -> o b"), y_row).then_inc(y_stored, 16)
            sp.wait_ge(y_stored, 16)

        @block.vector
        def _(dve):
            nc.vector.memset(w0_mirror[:, 0, :], 0.0)
            nc.vector.memset(w_raw[1][HALF:P, WIDE_CHUNKS - 1, :], 0.0)
            nc.vector.memset(w_raw[2][HALF:P, WIDE_CHUNKS - 1, :], 0.0).then_inc(pad_zero, 1)
            dve.wait_ge(cin_weights, 16 * 8)
            dve.wait_ge(pad_zero, 1)
            r = slice(0, PAIR_ROWS)
            nc.vector.tensor_tensor(w_raw[0][r, :, :], w_raw[0][r, :, :], w0_mirror[r, :, :],
                                    ALU.add).then_inc(w0_added, 1)
            dve.wait_ge(w0_added, 1)
            hi_steps = 0
            for layer in range(3):
                r = slice(0, P if layer else PAIR_ROWS)
                for u, c0, c1 in units(layer):
                    s0 = weight_slot(layer, c0)
                    s1 = s0 + c1 - c0
                    raw = w_raw[layer][r, c0:c1, :]
                    if kind_of(layer, u) == "full":
                        nc.vector.tensor_copy(w_full[layer][r, s0:s1, :], raw)
                        continue
                    hi, lo = w_hi[layer][r, s0:s1, :], w_lo[layer][r, s0:s1, :]
                    nc.vector.tensor_copy(hi, raw).then_inc(w_hi_made, 1)
                    hi_steps += 1
                    dve.wait_ge(w_hi_made, hi_steps)
                    nc.vector.tensor_tensor(lo, raw, hi.bitcast(F32), ALU.subtract)
            nc.vector.memset(part[:, :, :], 0.0).then_inc(weights_ready, 1)

            def products(b, j, layer, h, owed=None):
                r = slice(0, P if layer else PAIR_ROWS)
                for u, c0, c1 in units(layer):
                    if first(b) and j == 0 and layer == 0 and c0 == FIRST_PAIRS:
                        dve.wait_ge(pairs_loaded, 96)
                    if first(b) and j == 0 and layer == 1 and c0 == FIRST_WIDE:
                        dve.wait_ge(wide_loaded[0], 32)
                    n, kind = unit_no(b, j, layer, u), kind_of(layer, u)
                    fields = x_wide[r, j % 2, c0:c1, :] if layer else x_pairs[r, c0:c1, :]
                    by = h[r, :].unsqueeze(1).to_broadcast([r.stop, c1 - c0, TILE])
                    if kind == "full":
                        wait_slot_free(dve, used[kind], b, n, FULL_RING)
                        out = z_full[r, slot(b, j, layer, u, FULL_RING), 0:c1 - c0, :]
                    else:
                        wait_slot_free(dve, lo_made[kind], b, n, Z_RING[kind])
                        out = z_split[kind][r, slot(b, j, layer, u, Z_RING[kind]), 0:c1 - c0, :]
                    nc.vector.tensor_tensor(out, fields, by, ALU.mult).then_inc(made[kind], 1)
                    if owed:
                        make_lo(dve, *owed)
                    owed = (b, j, layer, u) if kind == "own" else None
                return owed

            def sum_tile(source, k, b, j):
                by_row = source.rearrange("p (d b) -> p b d", b=P)
                if j == 0:
                    nc.vector.tensor_reduce(block_sum[:, k, :], by_row, AX.X, ALU.add).then_inc(sums[k], 1)
                    return
                nc.vector.tensor_reduce(part[:, k, :], by_row, AX.X, ALU.add).then_inc(sums[k], 1)
                out = block_sum[:, k, :]
                if j == TILES - 1:
                    out = tower[:, k, LAST * P:BATCH] if last(b) else tower_out[:, k, :]
                    if not (first(b) or last(b)):
                        dve.wait_ge(tower_stored[k], b * 16)
                dve.wait_ge(sums[k], b * (2 * TILES - 1) + 2 * j)
                nc.vector.tensor_tensor(out, block_sum[:, k, :], part[:, k, :], ALU.add).then_inc(sums[k], 1)

            def sum_layer2(b, j):
                dve.wait_ge(out2, b * TILES + j + 1)
                sum_tile(direct2[:, :], 1, b, j)

            def sum_layers01(b, j):
                dve.wait_ge(out0, b * (3 * TILES) + 3 * j + 3)
                dve.wait_ge(out1, b * (3 * TILES) + 3 * j + 3)
                sum_tile(direct01[:, j % 2, :], 0, b, j)

            dve.wait_ge(x_again_made, 1)
            dve.wait_ge(first_pairs_loaded, 96)
            owed = products(0, 0, 0, x_again)
            if owed:
                make_lo(dve, *owed)

            def body(b):
                for j in range(TILES):
                    t3 = b * (3 * TILES) + 3 * j
                    dve.wait_ge(out0, t3 + 2)
                    if first(b) and j == 0:
                        dve.wait_ge(first_wide_loaded, 32)
                    else:
                        dve.wait_ge(wide_loaded[j % 2], b * (TILES * 16) + (j // 2 + 1) * 32)
                    owed = products(b, j, 1, h1)
                    if not (last(b) and j + 1 == TILES):
                        dve.wait_ge(pairs_loaded, b * (TILES * 96) + (j + 2) * 96)
                        dve.wait_ge(x_again_made, b * TILES + j + 2)
                        owed = products(b, j + 1, 0, x_again, owed)
                    if j:
                        sum_layer2(b, j - 1)
                    elif not first(b):
                        sum_layer2(b - 1, TILES - 1)
                    if owed:
                        make_lo(dve, *owed)
                    dve.wait_ge(out1, t3 + 2)
                    owed = products(b, j, 2, h2)
                    if owed:
                        make_lo(dve, *owed)
                    sum_layers01(b, j)

            over_blocks(dve, body)
            sum_layer2(LAST, TILES - 1)

        @block.tensor
        def _(pe):
            def transposes(b, j):
                n = b * TILES + j
                if not (first(b) and j < 2):
                    pe.wait_ge(x_copied, n - 1)
                    pe.sem_inc(x_bank_free, 1)
                bank_ = x_bank[j % 2]
                by_d = rows[:, :].rearrange("p (f d) -> p d f", d=DIM)
                for k in range(D_PER_TILE):
                    ins = nc.tensor.transpose(bank_[0:FIELDS, k * P:(k + 1) * P],
                                              by_d[:, j * D_PER_TILE + k, :], ident[:, :])
                ins.then_inc(transposed, 1)

            def contract(b, j, layer, acc):
                end = units(layer)[-1][0]

                def operands(c):
                    r = P if layer else pair_rows(c)
                    return slice(0, r), weight_slot(layer, c)

                def with_lo(u, c0, c1, final):
                    kind = kind_of(layer, u)
                    n, k = unit_no(b, j, layer, u), slot(b, j, layer, u, LO_RING[kind])
                    pe.wait_ge(lo_made[kind], n + 1)
                    for c in range(c0, c1):
                        r, w = operands(c)
                        ins = nc.tensor.matmul(acc[:, :], w_hi[layer][r, w, :], z_lo[kind][r, k, c - c0, :],
                                               start=False, stop=(final and c == c1 - 1))
                    ins.then_inc(used[kind], 1)

                owed = None
                for u, c0, c1 in units(layer):
                    n, kind = unit_no(b, j, layer, u), kind_of(layer, u)
                    if kind == "full":
                        k = slot(b, j, layer, u, FULL_RING)
                        pe.wait_ge(made[kind], n + 1)
                        for c in range(c0, c1):
                            r, w = operands(c)
                            ins = nc.tensor.matmul(acc[:, :], w_full[layer][r, w, :], z_full[r, k, c - c0, :],
                                                   start=(c == 0), stop=(u == end and not owed and c == c1 - 1))
                        ins.then_inc(used[kind], 1)
                    else:
                        k = slot(b, j, layer, u, HI_RING[kind])
                        pe.wait_ge(hi_made[kind], n + 1)
                        for c in range(c0, c1):
                            r, w = operands(c)
                            for part in (w_hi, w_lo):
                                nc.tensor.matmul(acc[:, :], part[layer][r, w, :], z_hi[kind][r, k, c - c0, :],
                                                 start=(c == 0 and part is w_hi), stop=False)
                    if owed:
                        with_lo(*owed, final=(u == end and kind == "full"))
                    owed = (u, c0, c1) if kind != "full" else None
                if owed:
                    with_lo(*owed, final=True)

            def top_layer1(q):
                if q == 0:
                    pe.wait_ge(biases_loaded, 16 * 6)
                    pe.wait_ge(top_weights, 16 * 4)
                    pe.wait_ge(tower_loaded, 32)
                    pe.wait_ge(x_copied, BLOCKS * TILES)
                    wait_z_made(pe, LAST, TILES - 1, 1)
                else:
                    pe.wait_ge(top1_out, 4 * q)
                if q == GROUPS - 1:
                    for k in range(2):
                        pe.wait_ge(sums[k], BLOCKS * (2 * TILES - 1))
                for m in range(TOP1 // P):
                    for k, (w, x) in enumerate(((wt1[:, 0, :], tower[:, 0, :]), (wt1_dense, dense),
                                                (wt1[:, 1, :], tower[:, 1, :]))):
                        ins = nc.tensor.matmul(top1_bank[m][:, :], w[:, m * P:(m + 1) * P],
                                               x[:, q * TILE:(q + 1) * TILE], start=(k == 0), stop=(k == 2))
                    ins.then_inc(top1_made, 1)

            def top_layer2(q):
                pe.wait_ge(top1_out, 4 * q + 4)
                if q:
                    pe.wait_ge(top2_out, 2 * q)
                else:
                    pe.wait_ge(out2, BLOCKS * TILES)
                    pe.wait_ge(out1, BLOCKS * TILES * 3)
                    pe.wait_ge(out0, BLOCKS * TILES * 3)
                for m in range(TOP2 // P):
                    for k in range(TOP1 // P):
                        ins = nc.tensor.matmul(top2_bank[m][:, :], wt2[:, k, m * P:(m + 1) * P],
                                               act1[:, k, :], start=(k == 0), stop=(k == TOP1 // P - 1))
                    ins.then_inc(top2_made, 1)

            def top_layer3(q):
                pe.wait_ge(top2_out, 2 * q + 2)
                if q:
                    pe.wait_ge(y_copied, q)
                else:
                    wait_z_made(pe, LAST, TILES - 1, 2)
                for k in range(TOP2 // P):
                    ins = nc.tensor.matmul(y_bank[0:1, :], wt3[:, k:k + 1], act2[:, k, :],
                                           start=(k == 0), stop=(k == TOP2 // P - 1))
                ins.then_inc(y_made, 1)

            pe.wait_ge(ident_ready, 1)
            pe.wait_ge(rows_moved, 1)
            for j in range(TILES):
                transposes(0, j)
            pe.wait_ge(weights_ready, 1)
            contract(0, 0, 0, acc0)

            def body(b):
                for j in range(TILES):
                    if j == TILES // 2 and not last(b):
                        pe.wait_ge(rows_moved, b + 2)
                    if j >= TILES // 2 and not last(b):
                        transposes(b + 1, 2 * j - TILES)
                        transposes(b + 1, 2 * j - TILES + 1)
                    if not (first(b) and j == 0):
                        pe.wait_ge(out1, b * (3 * TILES) + 3 * j)
                    contract(b, j, 1, acc1)
                    if last(b) and j + 1 == TILES:
                        top_layer1(0)
                    if not (last(b) and j + 1 == TILES):
                        pe.wait_ge(out0, b * (3 * TILES) + 3 * j + 3)
                        contract(b, j + 1, 0, acc0)
                    if not (first(b) and j == 0):
                        pe.wait_ge(out2, b * TILES + j)
                    contract(b, j, 2, acc2)

            over_blocks(pe, body)
            for q in range(GROUPS):
                top_layer2(q)
                if q + 1 < GROUPS:
                    top_layer1(q + 1)
                top_layer3(q)

        @block.scalar
        def _(act):
            def move_rows(b):
                act.wait_ge(gathered, b * (FIELDS * 16) + FIELDS * 16)
                if not first(b):
                    act.wait_ge(transposed, b * TILES)
                nc.scalar.activation(rows[:, :], rows_in[:, :], ACT.Copy).then_inc(rows_moved, 1)

            def take_x(b, j):
                n = b * TILES + j
                act.wait_ge(transposed, n + 1)
                if j >= 2:
                    act.wait_ge(x_stored[j - 2], b * 32 + 32)
                elif not first(b):
                    act.wait_ge(x_stored[j + 2], b * 32)
                nc.scalar.activation(x_out[:, j % 2, :], x_bank[j % 2][0:FIELDS, :], ACT.Copy).then_inc(x_copied, 1)

            def copy_x(b, j):
                if first(b) and j == 0:
                    act.wait_ge(first_pairs_loaded, 96)
                else:
                    act.wait_ge(pairs_loaded, b * (TILES * 96) + (j + 1) * 96)
                    pb, pj = (b, j - 1) if j else (b - 1, TILES - 1)
                    wait_z_made(act, pb, pj, 0)
                nc.scalar.activation(x_again[0:PAIR_ROWS, :], x_base[:, :], ACT.Copy).then_inc(x_again_made, 1)

            def round_z(b, j, layer, u):
                kind, (_, c0, c1), r = kind_of(layer, u), units(layer)[u], slice(0, P if layer else PAIR_ROWS)
                n, m = unit_no(b, j, layer, u), slice(0, c1 - c0)
                act.wait_ge(made[kind], n + 1)
                wait_slot_free(act, used[kind], b, n, HI_RING[kind])
                nc.scalar.activation(z_hi[kind][r, slot(b, j, layer, u, HI_RING[kind]), m, :],
                                     z_split[kind][r, slot(b, j, layer, u, Z_RING[kind]), m, :],
                                     ACT.Copy).then_inc(hi_made[kind], 1)

            def finish_layer(acc, bias, h, direct, done):
                low, high = slice(0, HALF), slice(HALF, P)
                nc.scalar.activation(h[low, :], acc[low, :], ACT.Relu, bias=bias[low, :]).then_inc(done, 1)
                nc.scalar.activation(h[high, :], acc[low, :], ACT.Relu, bias=bias[low, :]).then_inc(done, 1)
                nc.scalar.activation(direct, acc[high, :], ACT.Relu, bias=bias[high, :]).then_inc(done, 1)

            def finish0(b, j):
                wait_accumulated(act, b, j, 0)
                if j >= 2:
                    act.wait_ge(sums[0], b * (2 * TILES - 1) + (2 * j - 3))
                elif not first(b):
                    act.wait_ge(sums[0], b * (2 * TILES - 1) + (2 * j - 2))
                finish_layer(acc0, b0, h1, direct01[0:HALF, j % 2, :], out0)

            def finish1(b, j):
                wait_accumulated(act, b, j, 1)
                finish_layer(acc1, b1, h2, direct01[HALF:P, j % 2, :], out1)

            def finish2(b, j):
                wait_accumulated(act, b, j, 2)
                if j:
                    act.wait_ge(sums[1], b * (2 * TILES - 1) + (2 * j - 1))
                elif not first(b):
                    act.wait_ge(sums[1], b * (2 * TILES - 1))
                nc.scalar.activation(direct2[:, :], acc2[:, :], ACT.Relu, bias=b2[:, :]).then_inc(out2, 1)

            def finish_top1(q):
                for m in range(TOP1 // P):
                    act.wait_ge(top1_made, 4 * q + m + 1)
                    if q and m == 0:
                        act.wait_ge(top2_made, 2 * q)
                    nc.scalar.activation(act1[:, m, :], top1_bank[m][:, :], ACT.Relu,
                                         bias=bt1[:, m:m + 1]).then_inc(top1_out, 1)

            act.wait_ge(biases_loaded, 16 * 6)
            move_rows(0)
            for j in range(TILES):
                take_x(0, j)
            copy_x(0, 0)
            for u in split_units(0):
                round_z(0, 0, 0, u)
            finish0(0, 0)

            def body(b):
                for j in range(TILES):
                    if j == TILES // 2 and not last(b):
                        move_rows(b + 1)
                    if not (last(b) and j + 1 == TILES):
                        copy_x(b, j + 1)
                    for i, u in enumerate(split_units(1)):
                        if i == FINISH2_AT:
                            if j:
                                finish2(b, j - 1)
                            elif not first(b):
                                finish2(b - 1, TILES - 1)
                        if i == COPY_X_AT and j >= TILES // 2 and not last(b):
                            take_x(b + 1, 2 * j - TILES)
                            take_x(b + 1, 2 * j - TILES + 1)
                        round_z(b, j, 1, u)
                    if not (last(b) and j + 1 == TILES):
                        for u in split_units(0):
                            round_z(b, j + 1, 0, u)
                    finish1(b, j)
                    for i, u in enumerate(split_units(2)):
                        if i == FINISH0_AT:
                            if last(b) and j + 1 == TILES:
                                finish_top1(0)
                            else:
                                finish0(b, j + 1)
                        round_z(b, j, 2, u)

            over_blocks(act, body)
            finish2(LAST, TILES - 1)

            for q in range(GROUPS):
                for m in range(TOP2 // P):
                    act.wait_ge(top2_made, 2 * q + m + 1)
                    if q and m == 0:
                        act.wait_ge(y_made, q)
                    nc.scalar.activation(act2[:, m, :], top2_bank[m][:, :], ACT.Relu,
                                         bias=bt2[:, m:m + 1]).then_inc(top2_out, 1)
                if q + 1 < GROUPS:
                    finish_top1(q + 1)
                act.wait_ge(y_made, q + 1)
                nc.scalar.activation(y_row[:, q * TILE:(q + 1) * TILE], y_bank[0:1, :], ACT.Copy).then_inc(y_copied, 1)


def kernel(**inputs):
    import numpy as np
    import concourse.bacc as bacc
    from concourse.bass_utils import run_bass_kernel_spmd

    given = {k: np.ascontiguousarray(v) for k, v in inputs.items()}
    c, g, f = np.meshgrid(np.arange(PAIR_CHUNKS), np.arange(PAIR_GROUPS), np.arange(FIELDS), indexing="ij")
    partner = (f + np.vectorize(shift)(c, g)) % FIELDS
    shape = (PAIR_CHUNKS, PAIR_ROWS, P)
    W0 = given["L0_rec_W0"]
    arrays = {
        "ids": given["ids"],
        "dense": np.ascontiguousarray(given["dense_ctx"].T),
        "W0": W0[(f * FIELDS + partner).ravel()].reshape(shape),
        "W0_mirror": W0[(partner * FIELDS + f).ravel()].reshape(shape),
        "W1": given["L0_rec_W1"], "W2": given["L0_rec_W2"],
        "b0": given["L0_rec_b0"], "b1": given["L0_rec_b1"], "b2": given["L0_rec_b2"],
        "Wt1": given["W_top1"], "bt1": given["b_top1"], "Wt2": given["W_top2"], "bt2": given["b_top2"],
        "Wt3": given["W_top3"],
    }
    for i in range(FIELDS):
        arrays[f"tbl_{i}"] = given[f"tbl_{i}"]

    nc = bacc.Bacc("TRN2", target_bir_lowering=False, num_devices=1)
    t = {n: nc.dram_tensor(f"in_{n}", a.shape, mybir.dt.from_np(a.dtype), kind="ExternalInput").ap()
         for n, a in arrays.items()}
    t["ids"] = t["ids"].bitcast(U32)
    t["tbl"] = [t[f"tbl_{i}"] for i in range(FIELDS)]
    t["out"] = nc.dram_tensor("out_y", (BATCH, 1), F32, kind="ExternalOutput").ap()
    build(nc, t)
    r = run_bass_kernel_spmd(nc, [{f"in_{n}": a for n, a in arrays.items()}], core_ids=[0])
    return r.results[0]["out_y"]
```

```python
from contextlib import ExitStack

import concourse.bass as bass
from concourse import mybir

F32 = mybir.dt.float32
F32R = mybir.dt.float32r
U32 = mybir.dt.uint32
ALU = mybir.AluOpType
ACT = mybir.ActivationFunctionType
AX = mybir.AxisListType

FIELDS, DIM, BATCH = 39, 16, 2048
P = 128
HALF = 64
TILE = 512
BLOCKS = BATCH // P
TILES = P * DIM // TILE
COLS = BATCH * DIM
PAIR_CHUNKS = 7
PAIR_GROUPS = 3
PAIR_ROWS = PAIR_GROUPS * FIELDS
WIDE_CHUNKS = (FIELDS + 1) // 2
X_ROWS = FIELDS + PAIR_GROUPS * PAIR_CHUNKS - 1
D_PER_TILE = TILE // P
X_FIELDS = P // D_PER_TILE
X_PARTS = TILES + 1
X_REST = (FIELDS - X_FIELDS) * DIM
assert X_REST <= P
X_STORES = 2 * TILES + 1
CHUNKS = (PAIR_CHUNKS, WIDE_CHUNKS, WIDE_CHUNKS)
PLAN = (
    ((3, "full"), (2, "pool"), (2, "own")),
    ((2, "full"), (2, "pool"), (2, "own"), (2, "pool"), (3, "full"), (2, "pool"), (2, "own"),
     (2, "pool"), (3, "full")),
    ((3, "full"), (2, "pool"), (2, "own"), (2, "pool"), (2, "full"), (2, "pool"), (2, "own"),
     (2, "pool"), (3, "full")),
)
SPLIT_KINDS = ("pool", "own")
FULL_UNIT, SPLIT_UNIT = 3, 2
FULL_RING = 2
Z_RING = {"pool": 2, "own": 1}
HI_RING = {"pool": 3, "own": 1}
LO_RING = {"pool": 2, "own": 1}
TOP1, TOP2, DENSE = 512, 256, 16
GROUPS = BATCH // TILE
DENSE_AT = (0, 32, 64)
DENSE_ROWS = DENSE_AT[-1] + DENSE
LAST = BLOCKS - 1
COPY_X_AT, FINISH2_AT, TAKE_X_AT, FINISH0_AT = 5, 3, 4, 3
GATHERS = {2: (0, 1, 0, 3, 2, 0, 1, 0, 3), 3: (0, 1, 0, 3, 2, 0, 2, 0, 3),
           0: (0, 1, 0, 3, 2, 0, 2, 0, 3), 1: (0, 1, 0, 3, 3, 0, 0, 0, 0)}
AHEAD_GATHERS = sum(GATHERS[2]) + sum(GATHERS[3])
FIRST_GATHERS = 15


def pair_rows(c):
    return PAIR_ROWS if c < PAIR_CHUNKS - 1 else 2 * FIELDS


def shift(c, g):
    return 3 * c + (1, 0, 2)[g]


def units(layer):
    ends = [sum(n for n, _ in PLAN[layer][:u + 1]) for u in range(len(PLAN[layer]))]
    return [(u, end - PLAN[layer][u][0], end) for u, end in enumerate(ends)]


def kind_of(layer, u):
    return PLAN[layer][u][1]


def count(kind, order):
    return sum(kind_of(l, u) == kind for l, u in order)


def split_units(layer):
    return [u for u, _, _ in units(layer) if kind_of(layer, u) != "full"]


def weight_slot(layer, c):
    kinds = [kind_of(layer, u) == "full" for u, c0, c1 in units(layer) for _ in range(c0, c1)]
    return kinds[:c].count(kinds[c])


ORDER = [(l, u) for l in (1, 0, 2) for u, _, _ in units(l)]
ORDER0 = [(0, u) for u, _, _ in units(0)]
SPLIT_CHUNKS = [sum(c1 - c0 for u, c0, c1 in units(l) if kind_of(l, u) != "full") for l in range(3)]
FIRST_PAIRS = units(0)[0][2]
FIRST_WIDE = [c1 for _, _, c1 in units(1) if 2 * c1 >= WIDE_CHUNKS][0]
assert [units(l)[-1][2] for l in range(3)] == list(CHUNKS)
assert TILES * count("full", ORDER) % FULL_RING == 0
assert all(TILES * count(k, ORDER) % ring[k] == 0 for k in SPLIT_KINDS for ring in (Z_RING, HI_RING, LO_RING))
assert sum(map(sum, GATHERS.values())) == FIELDS
assert SPLIT_CHUNKS[1] >= 3 * TOP1 // P and SPLIT_CHUNKS[2] >= TOP1 // P * TOP2 // P
assert len(split_units(1)) > max(COPY_X_AT, FINISH2_AT, TAKE_X_AT) and len(split_units(2)) > FINISH0_AT


def build(nc, t):
    with ExitStack() as ctx:
        def sb(name, shape, dt=F32):
            return ctx.enter_context(nc.sbuf_tensor(name, shape, dt))

        def sem(name):
            return ctx.enter_context(nc.semaphore(name))

        ident = sb("ident", [P, P])
        ids_all = sb("ids_all", [P, BLOCKS, FIELDS], U32)
        ids = sb("ids_block", [P, FIELDS], U32)
        rows_in = sb("rows_in", [P, FIELDS * DIM])
        rows = sb("embedding_rows", [P, FIELDS * DIM])
        x_out = sb("x_out", [P, X_PARTS, P])
        x_base = sb("x_base", [PAIR_ROWS, TILE])
        x_pairs = sb("x_pairs", [PAIR_ROWS, PAIR_CHUNKS, TILE])
        x_wide = sb("x_wide", [P, 2, WIDE_CHUNKS, TILE])
        z_full = sb("z_full", [P, FULL_RING, FULL_UNIT, TILE])
        z_split = {k: sb(f"z_{k}", [P, Z_RING[k], SPLIT_UNIT, TILE]) for k in SPLIT_KINDS}
        z_hi = {k: sb(f"z_hi_{k}", [P, HI_RING[k], SPLIT_UNIT, TILE], F32R) for k in SPLIT_KINDS}
        z_lo = {k: sb(f"z_lo_{k}", [P, LO_RING[k], SPLIT_UNIT, TILE], F32R) for k in SPLIT_KINDS}
        w_full = [sb(f"w{l}_full", [P, CHUNKS[l] - SPLIT_CHUNKS[l], P]) for l in range(3)]
        w_hi = [sb(f"w{l}_hi", [P, SPLIT_CHUNKS[l], P], F32R) for l in range(3)]
        w_lo = [sb(f"w{l}_lo", [P, SPLIT_CHUNKS[l], P], F32R) for l in range(3)]
        b0 = sb("b0", [P, 1])
        b1 = sb("b1", [P, 1])
        b2 = sb("b2", [P, 1])
        bt1 = sb("bt1", [P, TOP1 // P])
        bt2 = sb("bt2", [P, TOP2 // P])
        wt3 = sb("wt3", [P, TOP2 // P])
        direct01 = sb("direct01", [P, 2, TILE])
        direct2 = sb("direct2", [P, TILE])
        part = sb("part", [P, 2, P])
        block_sum = sb("block_sum", [P, 2, P])
        tower_out = sb("tower_out", [P, 2, P])

        stage = x_wide[:, 1, :, :].rearrange("p c n -> p (c n)")
        at = 0
        w_raw = []
        for l in range(3):
            w_raw.append(stage[:, at:at + CHUNKS[l] * P].rearrange("p (c s) -> p c s", s=P))
            at += CHUNKS[l] * P
        w0_mirror = stage[:, at:at + PAIR_CHUNKS * P].rearrange("p (c s) -> p c s", s=P)

        late = x_pairs[:, :, :].rearrange("p c n -> p (c n)")
        stacked = late[0:DENSE_ROWS, 0:TOP1 + BATCH]
        wt1_dense_stack, dense_stack = stacked[:, 0:TOP1], stacked[:, TOP1:]
        wt1_dense, dense = wt1_dense_stack[0:DENSE, :], dense_stack[0:DENSE, :]
        free = x_wide[:, 0, :, :].rearrange("p c n -> p (c n)")
        wt1 = free[:, 0:2 * TOP1].rearrange("p (k s) -> p k s", k=2)
        wt2 = free[:, 2 * TOP1:4 * TOP1].rearrange("p (k s) -> p k s", k=TOP1 // P)
        tower = x_wide[:, 0, 4:4 + 2 * BATCH // TILE, :].rearrange("p c n -> p (c n)").rearrange(
            "p (k n) -> p k n", k=2)
        act1 = x_wide[:, 0, 12:12 + TOP1 // P, :]
        act2 = x_wide[:, 0, 16:16 + TOP2 // P, :]
        y_row = x_wide[0:1, 1, 0:GROUPS, :].rearrange("p a n -> p (a n)")

        wt1_hi, wt1_lo = (w[1][:, 0:2 * TOP1 // P, :].rearrange("p c s -> p (c s)").rearrange(
            "p (k s) -> p k s", k=2) for w in (w_hi, w_lo))
        wt2_hi, wt2_lo = (w[2][:, 0:TOP1 // P * TOP2 // P, :].rearrange("p c s -> p (c s)").rearrange(
            "p (k s) -> p k s", k=TOP1 // P) for w in (w_hi, w_lo))
        wt1_dense_parts = w_hi[1][0:DENSE_ROWS, 2 * TOP1 // P:3 * TOP1 // P, :].rearrange("p c s -> p (c s)")
        tower_hi, tower_lo = z_hi["pool"][:, 0, :, :], z_lo["own"][:, 0, :, :]
        dense_parts = z_hi["own"][0:DENSE_ROWS, 0, :, :]
        act1_hi = z_hi["pool"][:, 1:3, :, :].rearrange("p s m n -> p (s m) n")
        act1_lo = z_lo["pool"][:, :, :, :].rearrange("p s m n -> p (s m) n")

        bank = [ctx.enter_context(nc.psum_tensor(f"bank{i}", [P, TILE], F32)) for i in range(8)]
        acc0, acc1, acc2 = bank[0:3]
        x_bank = bank[3:5]
        h1, h2, x_again = bank[5:8]
        top1_bank = bank[3:6] + bank[7:8]
        top2_bank = bank[0:2]
        y_bank = bank[6]

        x_rows = nc.dram_tensor("x_rows", [X_ROWS, COLS], F32, kind="Internal").ap()
        tower_rows = nc.dram_tensor("tower_rows", [P, 2, BATCH], F32, kind="Internal").ap()

        ident_zero = sem("ident_zero")
        ident_ready = sem("ident_ready")
        cin_weights = sem("cin_weights_loaded")
        top_weights = sem("top_weights_loaded")
        biases_loaded = sem("biases_loaded")
        pad_zero = sem("pad_zero")
        w0_added = sem("w0_added")
        w_hi_made = sem("w_hi_made")
        weights_ready = sem("weights_ready")
        ids_loaded = sem("ids_loaded")
        ids_copied = sem("ids_copied")
        gather_may_start = sem("gather_may_start")
        rows_moved = sem("rows_moved")
        x_bank_free = sem("x_bank_free")
        gathered = sem("rows_gathered")
        transposed = sem("x_transposed")
        x_copied = sem("x_copied")
        x_stored = sem("x_stored")
        pairs_loaded = sem("x_pairs_loaded")
        first_pairs_loaded = sem("first_pairs_loaded")
        more_pairs_loaded = sem("more_pairs_loaded")
        first_wide_loaded = sem("first_wide_loaded")
        wide_loaded = [sem(f"x_wide_loaded{i}") for i in range(2)]
        made = {k: sem(f"{k}_products_made") for k in ("full", "pool", "own")}
        used = {k: sem(f"{k}_products_used") for k in ("full", "pool", "own")}
        hi_made = {k: sem(f"{k}_hi_made") for k in SPLIT_KINDS}
        lo_made = {k: sem(f"{k}_lo_made") for k in SPLIT_KINDS}
        x_again_made = sem("x_again_made")
        out0 = sem("layer0_out")
        out1 = sem("layer1_out")
        out2 = sem("layer2_out")
        sums = [sem(f"tower_sums{k}") for k in range(2)]
        tower_stored = [sem(f"tower_stored{k}") for k in range(2)]
        tower_loaded = sem("tower_loaded")
        dense_zero = sem("dense_zero")
        top_weights_hi = sem("top_weights_hi")
        top_weights_lo = sem("top_weights_lo")
        top_input_hi = sem("top_input_hi")
        top_input_lo = sem("top_input_lo")
        act1_hi_made = sem("act1_hi_made")
        act1_lo_made = sem("act1_lo_made")
        top1_made = sem("top1_made")
        top1_out = sem("top1_out")
        top2_made = sem("top2_made")
        top2_out = sem("top2_out")
        y_made = sem("y_made")
        y_copied = sem("y_copied")
        y_stored = sem("y_stored")

        block = ctx.enter_context(nc.Block())

        def over_blocks(eng, body):
            body(0)
            with eng.Fori(1, LAST) as b:
                body(b)
            body(LAST)

        def last(b):
            return isinstance(b, int) and b == LAST

        def first(b):
            return isinstance(b, int) and b == 0

        def x_window(row, row_step, count, rows_in, col, lead=None):
            outer = [COLS, rows_in] if lead is None else [0, lead]
            return bass.AP(x_rows.tensor, row * COLS + col, [outer, [row_step * COLS, count], [1, TILE]])

        def unit_no(b, j, layer, u):
            kind = kind_of(layer, u)
            if layer == 0:
                if first(b) and j == 0:
                    return count(kind, ORDER0[:u])
                j = j - 1
            n = count(kind, ORDER0) + j * count(kind, ORDER) + count(kind, ORDER[:ORDER.index((layer, u))])
            if last(b) and j == TILES - 1 and layer == 2:
                n -= count(kind, ORDER0)
            return n if first(b) else b * (TILES * count(kind, ORDER)) + n

        def slot(b, j, layer, u, ring):
            return unit_no(b if isinstance(b, int) else 1, j, layer, u) % ring

        def wait_slot_free(eng, sem_, b, n, ring):
            if not (first(b) and n < ring):
                eng.wait_ge(sem_, n + 1 - ring)

        def wait_z_made(eng, b, j, layer):
            u = units(layer)[-1][0]
            eng.wait_ge(made[kind_of(layer, u)], unit_no(b, j, layer, u) + 1)

        def wait_accumulated(eng, b, j, layer):
            u = units(layer)[-1][0]
            if kind_of(layer, u) == "full" and kind_of(layer, u - 1) != "full":
                u -= 1
            eng.wait_ge(used[kind_of(layer, u)], unit_no(b, j, layer, u) + 1)

        def make_lo(eng, b, j, layer, u):
            kind, (_, c0, c1), r = kind_of(layer, u), units(layer)[u], slice(0, P if layer else PAIR_ROWS)
            n, m = unit_no(b, j, layer, u), slice(0, c1 - c0)
            eng.wait_ge(hi_made[kind], n + 1)
            wait_slot_free(eng, used[kind], b, n, LO_RING[kind])
            eng.tensor_tensor(z_lo[kind][r, slot(b, j, layer, u, LO_RING[kind]), m, :],
                              z_split[kind][r, slot(b, j, layer, u, Z_RING[kind]), m, :],
                              z_hi[kind][r, slot(b, j, layer, u, HI_RING[kind]), m, :].bitcast(F32),
                              ALU.subtract).then_inc(lo_made[kind], 1)

        @block.gpsimd
        def _(pool):
            pool.memset(ident[:, :], 0.0).then_inc(ident_zero, 1)
            pool.wait_ge(ident_zero, 1)
            pool.affine_select(out=ident[:, :], in_=ident[:, :], compare_op=ALU.not_equal, fill=1.0,
                               base=0, pattern=[[-1, P]], channel_multiplier=1).then_inc(ident_ready, 1)

            def start_block(b):
                if not first(b):
                    pool.wait_ge(gathered, b * (FIELDS * 16))
                    pool.wait_ge(rows_moved, 2 * b)
                pool.sem_inc(gather_may_start, 1)
                nc.gpsimd.tensor_copy(ids[:, :], ids_all[:, bass.ds(b, 1), :].rearrange("p o f -> p (o f)")
                                      ).then_inc(ids_copied, 1)
                pool.wait_ge(ids_copied, b + 1)
                pool.sem_inc(gather_may_start, 1)

            def gather(b, fields):
                for f in fields:
                    pool.indirect_dma_start(
                        out=rows_in[:, f * DIM:(f + 1) * DIM], out_offset=None, in_=t["tbl"][f],
                        in_offset=bass.IndirectOffsetOnAxis(ap=ids[:, f:f + 1], axis=0),
                    ).then_inc(gathered, 16)

            pool.dma_start(ids_all[:, :, :], t["ids"].rearrange("(b p) f -> p b f", p=P)).then_inc(ids_loaded, 16)
            pool.wait_ge(ids_loaded, 16)
            start_block(0)
            gather(0, range(FIELDS))
            start_block(1)
            gather(1, range(FIRST_GATHERS))
            for l, u in ORDER0:
                if kind_of(l, u) == "pool":
                    make_lo(pool, 0, 0, 0, u)
            gather(1, range(FIRST_GATHERS, AHEAD_GATHERS))

            def body(b):
                for j in range(TILES):
                    ending = isinstance(b, int) and b >= LAST - 1
                    los = [(l, u) for l, u in ORDER if kind_of(l, u) == "pool"
                           and not (l == 0 and last(b) and j == TILES - 1)]
                    due = not (j >= TILES // 2 and ending or last(b))
                    done = {2: 0, 3: sum(GATHERS[2]), 0: AHEAD_GATHERS, 1: FIELDS - sum(GATHERS[1])}[j]
                    for i, (layer, u) in enumerate(los):
                        make_lo(pool, b, j + (layer == 0), layer, u)
                        if due and GATHERS[j][i]:
                            if j == TILES // 2 and not any(GATHERS[j][:i]):
                                start_block(b + 2)
                            gather(b + 2 if j >= TILES // 2 else b + 1, range(done, done + GATHERS[j][i]))
                            done += GATHERS[j][i]
                    if last(b) and j == TILES - 2:
                        wait_z_made(pool, LAST, TILES - 1, 0)
                        pool.memset(stacked, 0.0).then_inc(dense_zero, 1)

            body(0)
            with pool.Fori(1, LAST - 1) as b:
                body(b)
            body(LAST - 1)
            body(LAST)

        @block.sync
        def _(sp):
            sp.wait_ge(pad_zero, 1)
            sp.dma_start(w_raw[0][0:PAIR_ROWS, :, :], t["W0"].rearrange("c r s -> r c s")).then_inc(cin_weights, 16)
            mirror = t["W0_mirror"].rearrange("c r s -> r c s")
            for g in (0, 2):
                part = slice(g * FIELDS, (g + 1) * FIELDS)
                sp.dma_start(w0_mirror[part, 0, :], mirror[part, 0, :]).then_inc(cin_weights, 16)
            sp.dma_start(w0_mirror[0:PAIR_ROWS, 1:PAIR_CHUNKS, :],
                         mirror[:, 1:PAIR_CHUNKS, :]).then_inc(cin_weights, 16)
            full = (WIDE_CHUNKS - 1) * P
            for w, src in ((w_raw[1], t["W1"]), (w_raw[2], t["W2"])):
                sp.dma_start(w[:, 0:WIDE_CHUNKS - 1, :],
                             src[0:full, :].rearrange("(c r) s -> r c s", r=P)).then_inc(cin_weights, 16)
                sp.dma_start(w[0:HALF, WIDE_CHUNKS - 1, :], src[full:full + HALF, :]).then_inc(cin_weights, 16)
            for b, src in ((b0, t["b0"]), (b1, t["b1"]), (b2, t["b2"])):
                sp.dma_start(b[:, :], src.rearrange("(p o) -> p o", o=1)).then_inc(biases_loaded, 16)
            with nc.allow_non_contiguous_dma(reason="a few hundred words, once"):
                for dst, src in ((wt3, t["Wt3"].rearrange("(k r) o -> r (k o)", r=P)),
                                 (bt1, t["bt1"].rearrange("(k r) -> r k", r=P)),
                                 (bt2, t["bt2"].rearrange("(k r) -> r k", r=P))):
                    sp.dma_start(dst[:, :], src).then_inc(biases_loaded, 16)

            def load_first_pairs():
                sp.wait_ge(x_stored, 16 * 3)
                for c0, c1, done in ((0, FIRST_PAIRS, first_pairs_loaded),
                                     (FIRST_PAIRS, PAIR_CHUNKS, more_pairs_loaded)):
                    for g in range(PAIR_GROUPS):
                        part = slice(g * FIELDS, (g + 1) * FIELDS)
                        if c0 == 0:
                            sp.dma_start(x_base[part, :], x_rows[0:FIELDS, 0:TILE]).then_inc(done, 16)
                        sp.dma_start(x_pairs[part, c0:c1, :], x_window(shift(c0, g), 3, c1 - c0, FIELDS, 0)
                                     ).then_inc(done, 16)

            def load_pairs(b, j, col):
                if j == 0 or first(b):
                    sp.wait_ge(x_stored, b * (16 * X_STORES) + 16 * X_STORES)
                for g in range(PAIR_GROUPS):
                    part = slice(g * FIELDS, (g + 1) * FIELDS)
                    sp.dma_start(x_base[part, :], x_rows[0:FIELDS, bass.ds(col, TILE)]).then_inc(pairs_loaded, 16)
                    sp.dma_start(x_pairs[part, :, :], x_window(shift(0, g), 3, PAIR_CHUNKS, FIELDS, col)
                                 ).then_inc(pairs_loaded, 16)

            def load_wide(b, j, col, c0=0, c1=WIDE_CHUNKS, done=None):
                for odd in range(2):
                    sp.dma_start(x_wide[odd * HALF:(odd + 1) * HALF, j % 2, c0:c1, :],
                                 x_window(2 * c0 + odd, 2, c1 - c0, 0, col, lead=HALF)
                                 ).then_inc(done or wide_loaded[j % 2], 16)

            def store_tile(b, j):
                col = b * (P * DIM) + j * TILE
                for fields, row in ((X_FIELDS, 0), (X_ROWS - FIELDS, FIELDS)):
                    sp.dma_start(x_rows[row:row + fields, bass.ds(col, TILE)].rearrange("f (d n) -> f d n", n=P),
                                 x_out[0:fields * D_PER_TILE, j, :]).then_inc(x_stored, 16)

            def store_rest(b):
                sp.dma_start(x_rows[X_FIELDS:FIELDS, bass.ds(b * (P * DIM), P * DIM)].rearrange(
                    "f (d n) -> f d n", n=P), x_out[0:X_REST, TILES, :]).then_inc(x_stored, 16)

            sp.wait_ge(x_copied, 2)
            store_rest(0)
            store_tile(0, 0)
            load_first_pairs()
            load_wide(0, 0, 0, 0, FIRST_WIDE, first_wide_loaded)
            for j in range(1, TILES):
                store_tile(0, j)
            load_wide(0, 0, 0, FIRST_WIDE, WIDE_CHUNKS)

            def loads(b):
                for j in range(TILES):
                    if j == 1 and not first(b):
                        for k in range(2):
                            sp.wait_ge(sums[k], b * (2 * TILES - 1))
                            sp.dma_start(tower_rows[:, k, bass.ds((b - 1) * P, P)],
                                         tower_out[:, k, :]).then_inc(tower_stored[k], 16)
                    nb, nj = (b, j + 1) if j + 1 < TILES else (b + 1, 0)
                    if last(b) and j + 1 == TILES:
                        continue
                    col = b * (P * DIM) + (j + 1) * TILE
                    if j + 1 == TILES:
                        sp.wait_ge(x_copied, 2 * b + 4)
                        store_rest(b + 1)
                        for i in range(TILES):
                            store_tile(b + 1, i)
                    wait_z_made(sp, b, j, 0)
                    load_pairs(nb, nj, col)
                    if j:
                        wait_z_made(sp, b, j - 1, 2)
                    elif not first(b):
                        wait_z_made(sp, b - 1, TILES - 1, 2)
                    else:
                        sp.wait_ge(weights_ready, 1)
                    load_wide(nb, nj, col)

            over_blocks(sp, loads)
            wait_z_made(sp, LAST, TILES - 1, 0)
            sp.wait_ge(dense_zero, 1)
            for row in DENSE_AT:
                sp.dma_start(dense_stack[row:row + DENSE, :], t["dense"]).then_inc(top_weights, 16)
                sp.dma_start(wt1_dense_stack[row:row + DENSE, :],
                             t["Wt1"][2 * P:2 * P + DENSE, :]).then_inc(top_weights, 16)
            wait_z_made(sp, LAST, TILES - 2, 2)
            sp.dma_start(wt1, t["Wt1"][0:2 * P, :].rearrange("(k r) s -> r k s", r=P)).then_inc(top_weights, 16)
            sp.dma_start(wt2, t["Wt2"].rearrange("(k r) s -> r k s", r=P)).then_inc(top_weights, 16)
            for k in range(2):
                sp.wait_ge(tower_stored[k], LAST * 16)
                sp.dma_start(tower[:, k, 0:LAST * P], tower_rows[:, k, 0:LAST * P]).then_inc(tower_loaded, 16)
            sp.wait_ge(y_copied, GROUPS)
            sp.dma_start(t["out"].rearrange("b o -> o b"), y_row).then_inc(y_stored, 16)
            sp.wait_ge(y_stored, 16)

        @block.vector
        def _(dve):
            nc.vector.memset(w0_mirror[:, 0, :], 0.0)
            nc.vector.memset(w_raw[1][HALF:P, WIDE_CHUNKS - 1, :], 0.0)
            nc.vector.memset(w_raw[2][HALF:P, WIDE_CHUNKS - 1, :], 0.0).then_inc(pad_zero, 1)
            dve.wait_ge(cin_weights, 16 * 8)
            dve.wait_ge(pad_zero, 1)
            r = slice(0, PAIR_ROWS)
            nc.vector.tensor_tensor(w_raw[0][r, :, :], w_raw[0][r, :, :], w0_mirror[r, :, :],
                                    ALU.add).then_inc(w0_added, 1)
            dve.wait_ge(w0_added, 1)
            hi_steps = 0
            for layer in range(3):
                r = slice(0, P if layer else PAIR_ROWS)
                for u, c0, c1 in units(layer):
                    s0 = weight_slot(layer, c0)
                    s1 = s0 + c1 - c0
                    raw = w_raw[layer][r, c0:c1, :]
                    if kind_of(layer, u) == "full":
                        nc.vector.tensor_copy(w_full[layer][r, s0:s1, :], raw)
                        continue
                    hi, lo = w_hi[layer][r, s0:s1, :], w_lo[layer][r, s0:s1, :]
                    nc.vector.tensor_copy(hi, raw).then_inc(w_hi_made, 1)
                    hi_steps += 1
                    dve.wait_ge(w_hi_made, hi_steps)
                    nc.vector.tensor_tensor(lo, raw, hi.bitcast(F32), ALU.subtract)
            nc.vector.memset(part[:, :, :], 0.0).then_inc(weights_ready, 1)

            def products(b, j, layer, h, owed=None):
                r = slice(0, P if layer else PAIR_ROWS)
                for u, c0, c1 in units(layer):
                    if first(b) and j == 0 and layer == 0 and c0 == FIRST_PAIRS:
                        dve.wait_ge(more_pairs_loaded, 48)
                    if first(b) and j == 0 and layer == 1 and c0 == FIRST_WIDE:
                        dve.wait_ge(wide_loaded[0], 32)
                    n, kind = unit_no(b, j, layer, u), kind_of(layer, u)
                    fields = x_wide[r, j % 2, c0:c1, :] if layer else x_pairs[r, c0:c1, :]
                    by = h[r, :].unsqueeze(1).to_broadcast([r.stop, c1 - c0, TILE])
                    if kind == "full":
                        wait_slot_free(dve, used[kind], b, n, FULL_RING)
                        out = z_full[r, slot(b, j, layer, u, FULL_RING), 0:c1 - c0, :]
                    else:
                        wait_slot_free(dve, lo_made[kind], b, n, Z_RING[kind])
                        out = z_split[kind][r, slot(b, j, layer, u, Z_RING[kind]), 0:c1 - c0, :]
                    nc.vector.tensor_tensor(out, fields, by, ALU.mult).then_inc(made[kind], 1)
                    if owed:
                        make_lo(dve, *owed)
                    owed = (b, j, layer, u) if kind == "own" else None
                return owed

            def sum_tile(source, k, b, j):
                by_row = source.rearrange("p (d b) -> p b d", b=P)
                if j == 0:
                    nc.vector.tensor_reduce(block_sum[:, k, :], by_row, AX.X, ALU.add).then_inc(sums[k], 1)
                    return
                nc.vector.tensor_reduce(part[:, k, :], by_row, AX.X, ALU.add).then_inc(sums[k], 1)
                out = block_sum[:, k, :]
                if j == TILES - 1:
                    out = tower[:, k, LAST * P:BATCH] if last(b) else tower_out[:, k, :]
                    if not (first(b) or last(b)):
                        dve.wait_ge(tower_stored[k], b * 16)
                dve.wait_ge(sums[k], b * (2 * TILES - 1) + 2 * j)
                nc.vector.tensor_tensor(out, block_sum[:, k, :], part[:, k, :], ALU.add).then_inc(sums[k], 1)

            def sum_layer2(b, j):
                dve.wait_ge(out2, b * TILES + j + 1)
                sum_tile(direct2[:, :], 1, b, j)

            def sum_layers01(b, j):
                dve.wait_ge(out0, b * (3 * TILES) + 3 * j + 3)
                dve.wait_ge(out1, b * (3 * TILES) + 3 * j + 3)
                sum_tile(direct01[:, j % 2, :], 0, b, j)

            dve.wait_ge(x_again_made, 1)
            dve.wait_ge(first_pairs_loaded, 96)
            owed = products(0, 0, 0, x_again)
            if owed:
                make_lo(dve, *owed)

            def body(b):
                for j in range(TILES):
                    t3 = b * (3 * TILES) + 3 * j
                    dve.wait_ge(out0, t3 + 2)
                    if first(b) and j == 0:
                        dve.wait_ge(first_wide_loaded, 32)
                    else:
                        dve.wait_ge(wide_loaded[j % 2], b * (TILES * 16) + (j // 2 + 1) * 32)
                    owed = products(b, j, 1, h1)
                    if not (last(b) and j + 1 == TILES):
                        dve.wait_ge(pairs_loaded, b * (TILES * 96) + (j + 1) * 96)
                        dve.wait_ge(x_again_made, b * TILES + j + 2)
                        owed = products(b, j + 1, 0, x_again, owed)
                    if j:
                        sum_layer2(b, j - 1)
                    elif not first(b):
                        sum_layer2(b - 1, TILES - 1)
                    if owed:
                        make_lo(dve, *owed)
                    dve.wait_ge(out1, t3 + 2)
                    owed = products(b, j, 2, h2)
                    if owed:
                        make_lo(dve, *owed)
                    sum_layers01(b, j)

            over_blocks(dve, body)

            def flat(x):
                return x.rearrange("p k n -> p (k n)")

            def lo_of(out, full, hi, done):
                nc.vector.tensor_tensor(out, full, hi.bitcast(F32), ALU.subtract).then_inc(done, 1)

            def input_lo(q):
                cols = slice(q * TILE, (q + 1) * TILE)
                low = slice(DENSE_AT[1], DENSE_AT[1] + DENSE)
                dve.wait_ge(top_input_hi, 2 * q - 1)
                lo_of(tower_lo, tower[:, :, cols], tower_hi, top_input_lo)
                dve.wait_ge(top_input_hi, 2 * q)
                lo_of(dense_parts[low, q % 2, :], dense_stack[low, cols], dense_parts[low, q % 2, :], top_input_lo)

            low = slice(DENSE_AT[2], DENSE_AT[2] + DENSE)
            dve.wait_ge(top_weights_hi, 1)
            lo_of(flat(wt1_lo), flat(wt1), flat(wt1_hi), top_weights_lo)
            dve.wait_ge(top_weights_hi, 2)
            lo_of(wt1_dense_parts[low, :], wt1_dense_stack[low, :], wt1_dense_parts[low, :], top_weights_lo)
            sum_layer2(LAST, TILES - 1)
            input_lo(1)
            dve.wait_ge(top_weights_hi, 3)
            lo_of(flat(wt2_lo), flat(wt2), flat(wt2_hi), top_weights_lo)
            for q in range(1, GROUPS):
                for m in range(TOP1 // P):
                    dve.wait_ge(act1_hi_made, 4 * (q - 1) + m + 1)
                    lo_of(act1_lo[:, m, :], act1[:, m, :], act1_hi[:, m, :], act1_lo_made)
                if q + 1 < GROUPS:
                    input_lo(q + 1)

        @block.tensor
        def _(pe):
            def transposes(b):
                if not first(b):
                    pe.wait_ge(x_copied, 2 * b)
                pe.wait_ge(rows_moved, 2 * b + 2)
                pe.sem_inc(x_bank_free, 1)
                nc.tensor.transpose(x_bank[1][0:X_REST, 0:P], rows[:, TILES * P:], ident[:, :])
                for i in range(TILES):
                    ins = nc.tensor.transpose(x_bank[0][:, i * P:(i + 1) * P], rows[:, i * P:(i + 1) * P], ident[:, :])
                ins.then_inc(transposed, 1)

            def contract(b, j, layer, acc):
                end = units(layer)[-1][0]

                def operands(c):
                    r = P if layer else pair_rows(c)
                    return slice(0, r), weight_slot(layer, c)

                def with_lo(u, c0, c1, final):
                    kind = kind_of(layer, u)
                    n, k = unit_no(b, j, layer, u), slot(b, j, layer, u, LO_RING[kind])
                    pe.wait_ge(lo_made[kind], n + 1)
                    for c in range(c0, c1):
                        r, w = operands(c)
                        ins = nc.tensor.matmul(acc[:, :], w_hi[layer][r, w, :], z_lo[kind][r, k, c - c0, :],
                                               start=False, stop=(final and c == c1 - 1))
                    ins.then_inc(used[kind], 1)

                owed = None
                for u, c0, c1 in units(layer):
                    n, kind = unit_no(b, j, layer, u), kind_of(layer, u)
                    if kind == "full":
                        k = slot(b, j, layer, u, FULL_RING)
                        pe.wait_ge(made[kind], n + 1)
                        for c in range(c0, c1):
                            r, w = operands(c)
                            ins = nc.tensor.matmul(acc[:, :], w_full[layer][r, w, :], z_full[r, k, c - c0, :],
                                                   start=(c == 0), stop=(u == end and not owed and c == c1 - 1))
                        ins.then_inc(used[kind], 1)
                    else:
                        k = slot(b, j, layer, u, HI_RING[kind])
                        pe.wait_ge(hi_made[kind], n + 1)
                        for c in range(c0, c1):
                            r, w = operands(c)
                            for part in (w_hi, w_lo):
                                nc.tensor.matmul(acc[:, :], part[layer][r, w, :], z_hi[kind][r, k, c - c0, :],
                                                 start=(c == 0 and part is w_hi), stop=False)
                    if owed:
                        with_lo(*owed, final=(u == end and kind == "full"))
                    owed = (u, c0, c1) if kind != "full" else None
                if owed:
                    with_lo(*owed, final=True)

            def top_layer1(q):
                if q == 0:
                    pe.wait_ge(biases_loaded, 16 * 6)
                    pe.wait_ge(top_weights, 16 * 8)
                    pe.wait_ge(tower_loaded, 32)
                    pe.wait_ge(x_copied, 2 * BLOCKS)
                    wait_z_made(pe, LAST, TILES - 1, 1)
                else:
                    pe.wait_ge(top1_out, 4 * q)
                    if q > 1:
                        pe.wait_ge(act1_hi_made, 4 * (q - 1))
                    pe.wait_ge(top_input_hi, 2 * q)
                    pe.wait_ge(top_input_lo, 2 * q)
                    pe.wait_ge(top_weights_lo, 2)
                cols = slice(q * TILE, (q + 1) * TILE)
                if q == 0:
                    passes = ((wt1[:, 0, :], tower[:, 0, cols]), (wt1[:, 1, :], tower[:, 1, cols]),
                              (wt1_dense, dense[:, cols]))
                else:
                    passes = [(w[:, k, :], x[:, k, :]) for w, x in ((wt1_hi, tower_hi), (wt1_lo, tower_hi),
                                                                    (wt1_hi, tower_lo)) for k in range(2)]
                    passes.append((wt1_dense_parts, dense_parts[:, q % 2, :]))
                for m in range(TOP1 // P):
                    for i, (w, x) in enumerate(passes):
                        ins = nc.tensor.matmul(top1_bank[m][:, :], w[:, m * P:(m + 1) * P], x,
                                               start=(i == 0), stop=(i == len(passes) - 1))
                    ins.then_inc(top1_made, 1)

            def top_layer2(q):
                if q:
                    pe.wait_ge(top2_out, 2 * q)
                    pe.wait_ge(top_weights_lo, 3)
                else:
                    pe.wait_ge(top1_out, 4)
                    pe.wait_ge(out2, BLOCKS * TILES)
                    pe.wait_ge(out1, BLOCKS * TILES * 3)
                    pe.wait_ge(out0, BLOCKS * TILES * 3)
                steps = TOP1 // P
                for m in range(TOP2 // P):
                    out = slice(m * P, (m + 1) * P)
                    for k in range(steps):
                        if q == 0:
                            ins = nc.tensor.matmul(top2_bank[m][:, :], wt2[:, k, out], act1[:, k, :],
                                                   start=(k == 0), stop=(k == steps - 1))
                            continue
                        if m == 0:
                            pe.wait_ge(act1_hi_made, 4 * (q - 1) + k + 1)
                        for w in (wt2_hi, wt2_lo):
                            nc.tensor.matmul(top2_bank[m][:, :], w[:, k, out], act1_hi[:, k, :],
                                             start=(k == 0 and w is wt2_hi), stop=False)
                    for k in range(steps if q else 0):
                        if m == 0:
                            pe.wait_ge(act1_lo_made, 4 * (q - 1) + k + 1)
                        ins = nc.tensor.matmul(top2_bank[m][:, :], wt2_hi[:, k, out], act1_lo[:, k, :],
                                               start=False, stop=(k == steps - 1))
                    ins.then_inc(top2_made, 1)

            def top_layer3(q):
                pe.wait_ge(top2_out, 2 * q + 2)
                if q:
                    pe.wait_ge(y_copied, q)
                else:
                    wait_z_made(pe, LAST, TILES - 1, 2)
                for k in range(TOP2 // P):
                    ins = nc.tensor.matmul(y_bank[0:1, :], wt3[:, k:k + 1], act2[:, k, :],
                                           start=(k == 0), stop=(k == TOP2 // P - 1))
                ins.then_inc(y_made, 1)

            pe.wait_ge(ident_ready, 1)
            transposes(0)
            pe.wait_ge(weights_ready, 1)
            contract(0, 0, 0, acc0)

            def body(b):
                for j in range(TILES):
                    if j == TILES // 2 and not last(b):
                        transposes(b + 1)
                    if not (first(b) and j == 0):
                        pe.wait_ge(out1, b * (3 * TILES) + 3 * j)
                    contract(b, j, 1, acc1)
                    if last(b) and j + 1 == TILES:
                        top_layer1(0)
                    if not (last(b) and j + 1 == TILES):
                        pe.wait_ge(out0, b * (3 * TILES) + 3 * j + 3)
                        contract(b, j + 1, 0, acc0)
                    if not (first(b) and j == 0):
                        pe.wait_ge(out2, b * TILES + j)
                    contract(b, j, 2, acc2)

            over_blocks(pe, body)
            for q in range(GROUPS):
                top_layer2(q)
                if q + 1 < GROUPS:
                    top_layer1(q + 1)
                top_layer3(q)

        @block.scalar
        def _(act):
            def move_rows(b):
                act.wait_ge(gathered, b * (FIELDS * 16) + FIELDS * 16)
                if not first(b):
                    act.wait_ge(transposed, b)
                by_tile = rows_in[:, :].rearrange("p (f t k) -> p t f k", t=TILES, k=D_PER_TILE)
                nc.scalar.activation(rows[:, X_FIELDS * DIM:], rows_in[:, X_FIELDS * DIM:], ACT.Copy
                                     ).then_inc(rows_moved, 1)
                nc.scalar.activation(rows[:, 0:X_FIELDS * DIM].rearrange("p (t f k) -> p t f k", t=TILES, k=D_PER_TILE),
                                     by_tile[:, :, 0:X_FIELDS, :], ACT.Copy).then_inc(rows_moved, 1)

            def take_x(b):
                act.wait_ge(transposed, b + 1)
                if not first(b):
                    act.wait_ge(x_stored, b * (16 * X_STORES))
                nc.scalar.activation(x_out[0:X_REST, TILES, :], x_bank[1][0:X_REST, 0:P], ACT.Copy).then_inc(x_copied, 1)
                nc.scalar.activation(x_out[:, 0:TILES, :].rearrange("p i n -> p (i n)"), x_bank[0][:, :],
                                     ACT.Copy).then_inc(x_copied, 1)

            def copy_x(b, j):
                if first(b) and j == 0:
                    act.wait_ge(first_pairs_loaded, 96)
                else:
                    act.wait_ge(pairs_loaded, b * (TILES * 96) + j * 96)
                    pb, pj = (b, j - 1) if j else (b - 1, TILES - 1)
                    wait_z_made(act, pb, pj, 0)
                nc.scalar.activation(x_again[0:PAIR_ROWS, :], x_base[:, :], ACT.Copy).then_inc(x_again_made, 1)

            def round_z(b, j, layer, u):
                kind, (_, c0, c1), r = kind_of(layer, u), units(layer)[u], slice(0, P if layer else PAIR_ROWS)
                n, m = unit_no(b, j, layer, u), slice(0, c1 - c0)
                act.wait_ge(made[kind], n + 1)
                wait_slot_free(act, used[kind], b, n, HI_RING[kind])
                nc.scalar.activation(z_hi[kind][r, slot(b, j, layer, u, HI_RING[kind]), m, :],
                                     z_split[kind][r, slot(b, j, layer, u, Z_RING[kind]), m, :],
                                     ACT.Copy).then_inc(hi_made[kind], 1)

            def finish_layer(acc, bias, h, direct, done):
                low, high = slice(0, HALF), slice(HALF, P)
                nc.scalar.activation(h[low, :], acc[low, :], ACT.Relu, bias=bias[low, :]).then_inc(done, 1)
                nc.scalar.activation(h[high, :], acc[low, :], ACT.Relu, bias=bias[low, :]).then_inc(done, 1)
                nc.scalar.activation(direct, acc[high, :], ACT.Relu, bias=bias[high, :]).then_inc(done, 1)

            def finish0(b, j):
                wait_accumulated(act, b, j, 0)
                if j >= 2:
                    act.wait_ge(sums[0], b * (2 * TILES - 1) + (2 * j - 3))
                elif not first(b):
                    act.wait_ge(sums[0], b * (2 * TILES - 1) + (2 * j - 2))
                finish_layer(acc0, b0, h1, direct01[0:HALF, j % 2, :], out0)

            def finish1(b, j):
                wait_accumulated(act, b, j, 1)
                finish_layer(acc1, b1, h2, direct01[HALF:P, j % 2, :], out1)

            def finish2(b, j):
                wait_accumulated(act, b, j, 2)
                if j:
                    act.wait_ge(sums[1], b * (2 * TILES - 1) + (2 * j - 1))
                elif not first(b):
                    act.wait_ge(sums[1], b * (2 * TILES - 1))
                nc.scalar.activation(direct2[:, :], acc2[:, :], ACT.Relu, bias=b2[:, :]).then_inc(out2, 1)

            def finish_top1(q):
                for m in range(TOP1 // P):
                    act.wait_ge(top1_made, 4 * q + m + 1)
                    if q and m == 0:
                        act.wait_ge(top2_made, 2 * q)
                        if q > 1:
                            act.wait_ge(act1_lo_made, 4 * (q - 1))
                    nc.scalar.activation(act1[:, m, :], top1_bank[m][:, :], ACT.Relu,
                                         bias=bt1[:, m:m + 1]).then_inc(top1_out, 1)
                    if q:
                        nc.scalar.activation(act1_hi[:, m, :], top1_bank[m][:, :], ACT.Relu,
                                             bias=bt1[:, m:m + 1]).then_inc(act1_hi_made, 1)

            def flat(x):
                return x.rearrange("p k n -> p (k n)")

            def input_hi(q):
                cols = slice(q * TILE, (q + 1) * TILE)
                if q > 1:
                    act.wait_ge(top1_made, 4 * q)
                if q == GROUPS - 1:
                    for k in range(2):
                        act.wait_ge(sums[k], BLOCKS * (2 * TILES - 1))
                nc.scalar.activation(tower_hi, tower[:, :, cols], ACT.Copy).then_inc(top_input_hi, 1)
                nc.scalar.activation(dense_parts[:, q % 2, :], dense_stack[:, cols], ACT.Copy
                                     ).then_inc(top_input_hi, 1)

            act.wait_ge(biases_loaded, 16 * 6)
            move_rows(0)
            take_x(0)
            copy_x(0, 0)
            for u in split_units(0):
                round_z(0, 0, 0, u)
            finish0(0, 0)

            def body(b):
                for j in range(TILES):
                    if j == TILES // 2 and not last(b):
                        move_rows(b + 1)
                    for i, u in enumerate(split_units(1)):
                        if i == COPY_X_AT and not (last(b) and j + 1 == TILES):
                            copy_x(b, j + 1)
                        if i == FINISH2_AT:
                            if j:
                                finish2(b, j - 1)
                            elif not first(b):
                                finish2(b - 1, TILES - 1)
                        if i == TAKE_X_AT and j == TILES // 2 and not last(b):
                            take_x(b + 1)
                        round_z(b, j, 1, u)
                    if not (last(b) and j + 1 == TILES):
                        for u in split_units(0):
                            round_z(b, j + 1, 0, u)
                    finish1(b, j)
                    for i, u in enumerate(split_units(2)):
                        if i == FINISH0_AT:
                            if last(b) and j + 1 == TILES:
                                finish_top1(0)
                            else:
                                finish0(b, j + 1)
                        round_z(b, j, 2, u)

            over_blocks(act, body)
            act.wait_ge(top_weights, 16 * 8)
            nc.scalar.activation(flat(wt1_hi), flat(wt1), ACT.Copy).then_inc(top_weights_hi, 1)
            nc.scalar.activation(wt1_dense_parts, wt1_dense_stack, ACT.Copy).then_inc(top_weights_hi, 1)
            finish2(LAST, TILES - 1)
            act.wait_ge(tower_loaded, 32)
            input_hi(1)
            nc.scalar.activation(flat(wt2_hi), flat(wt2), ACT.Copy).then_inc(top_weights_hi, 1)

            for q in range(GROUPS):
                for m in range(TOP2 // P):
                    act.wait_ge(top2_made, 2 * q + m + 1)
                    if q and m == 0:
                        act.wait_ge(y_made, q)
                    nc.scalar.activation(act2[:, m, :], top2_bank[m][:, :], ACT.Relu,
                                         bias=bt2[:, m:m + 1]).then_inc(top2_out, 1)
                if q + 1 < GROUPS:
                    finish_top1(q + 1)
                if q + 2 < GROUPS:
                    input_hi(q + 2)
                act.wait_ge(y_made, q + 1)
                nc.scalar.activation(y_row[:, q * TILE:(q + 1) * TILE], y_bank[0:1, :], ACT.Copy).then_inc(y_copied, 1)


def kernel(**inputs):
    import numpy as np
    import concourse.bacc as bacc
    from concourse.bass_utils import run_bass_kernel_spmd

    given = {k: np.ascontiguousarray(v) for k, v in inputs.items()}
    c, g, f = np.meshgrid(np.arange(PAIR_CHUNKS), np.arange(PAIR_GROUPS), np.arange(FIELDS), indexing="ij")
    partner = (f + np.vectorize(shift)(c, g)) % FIELDS
    shape = (PAIR_CHUNKS, PAIR_ROWS, P)
    W0 = given["L0_rec_W0"]
    arrays = {
        "ids": given["ids"],
        "dense": np.ascontiguousarray(given["dense_ctx"].T),
        "W0": W0[(f * FIELDS + partner).ravel()].reshape(shape),
        "W0_mirror": W0[(partner * FIELDS + f).ravel()].reshape(shape),
        "W1": given["L0_rec_W1"], "W2": given["L0_rec_W2"],
        "b0": given["L0_rec_b0"], "b1": given["L0_rec_b1"], "b2": given["L0_rec_b2"],
        "Wt1": given["W_top1"], "bt1": given["b_top1"], "Wt2": given["W_top2"], "bt2": given["b_top2"],
        "Wt3": given["W_top3"],
    }
    for i in range(FIELDS):
        arrays[f"tbl_{i}"] = given[f"tbl_{i}"]

    nc = bacc.Bacc("TRN2", target_bir_lowering=False, num_devices=1)
    t = {n: nc.dram_tensor(f"in_{n}", a.shape, mybir.dt.from_np(a.dtype), kind="ExternalInput").ap()
         for n, a in arrays.items()}
    t["ids"] = t["ids"].bitcast(U32)
    t["tbl"] = [t[f"tbl_{i}"] for i in range(FIELDS)]
    t["out"] = nc.dram_tensor("out_y", (BATCH, 1), F32, kind="ExternalOutput").ap()
    build(nc, t)
    r = run_bass_kernel_spmd(nc, [{f"in_{n}": a for n, a in arrays.items()}], core_ids=[0])
    return r.results[0]["out_y"]
```
